# Optimizing a Trainium2 kernel written in Bass

```python
import numpy as np
import jax
import jax.numpy as jnp

def _softmax(x, axis=-1):
    return jax.nn.softmax(x, axis=axis)
def _gelu(x):
    return jax.nn.gelu(x, approximate=True)
def _silu(x):
    return jax.nn.silu(x)
def _sigmoid(x):
    return jax.nn.sigmoid(x)
def _layernorm(x, axis=-1, eps=1e-5):
    m = jnp.mean(x, axis=axis, keepdims=True)
    v = jnp.var(x, axis=axis, keepdims=True)
    return (x - m) / jnp.sqrt(v + eps)
def _scatter_add(tgt, idx, src, axis=0):
    return tgt.at[idx].add(src)
def _segment_sum(src, seg, n):
    return jax.ops.segment_sum(src, seg, n)

kernel_name = 'mk_adj_resnorm_d1_adj_1024_13214b'

def setup_inputs(seed: int = 0):
    np.random.seed(seed)
    _w = jnp.asarray
    def _rec_inputs():
        import jax
        import jax.numpy as jnp
        _gk = jax.random.key(seed)
        x = -0.000125 + 0.9999 * jax.random.normal(jax.random.fold_in(_gk, 1), (16, 1024, 1024), jnp.float32)
        _a = jax.random.bernoulli(jax.random.fold_in(_gk, 2), 0.03125, (16, 1024, 1024))
        _a = jnp.logical_or(_a, jnp.swapaxes(_a, -1, -2))
        _a = jnp.logical_or(_a, jnp.eye(1024, dtype=bool))
        _af = _a.astype(jnp.float32)
        _af = _af * jax.random.uniform(jax.random.fold_in(_gk, 3), (16, 1024, 1024), jnp.float32, 0.05, 0.999994)
        adj = _af
        return x, adj
    x, adj = _rec_inputs()
    def _L0_gnn_setup():
        import jax, jax.numpy as jnp
        import numpy as np
        B, N, H, E = (64, 512, 1024, 4)
        BN_EPS = 1e-05
        key = jax.random.key(seed)
        ks = jax.random.split(key, 6)
        x = jax.random.normal(ks[0], (B, N, H), dtype=jnp.float32)
        adj = jax.random.uniform(ks[1], (B, N, N), dtype=jnp.float32)
        stdv = 1.0 / np.sqrt(H)
        expert_w = jax.random.uniform(ks[2], (E, H, H), minval=-stdv, maxval=stdv, dtype=jnp.float32)
        r_std = 1.0 / np.sqrt(H)
        router_w = jax.random.uniform(ks[3], (H, E), minval=-r_std, maxval=r_std, dtype=jnp.float32)
        router_b = jax.random.uniform(ks[4], (E,), minval=-r_std, maxval=r_std, dtype=jnp.float32)
        bn_gamma = jnp.ones((E, H), dtype=jnp.float32)
        bn_beta = jnp.zeros((E, H), dtype=jnp.float32)
        return {'x': x, 'adj': adj, 'router_w': router_w, 'router_b': router_b, 'expert_w': expert_w, 'bn_gamma': bn_gamma, 'bn_beta': bn_beta}
    _L0_gnn_all = _L0_gnn_setup()
    _L0_gnn_in = {k: v for k, v in _L0_gnn_all.items() if k in ('router_w', 'router_b', 'expert_w', 'bn_gamma', 'bn_beta', )}
    del _L0_gnn_all

    return {
        "x": x,
        "adj": adj,
        "L0_gnn_router_w": _L0_gnn_in["router_w"],
        "L0_gnn_router_b": _L0_gnn_in["router_b"],
        "L0_gnn_expert_w": _L0_gnn_in["expert_w"],
        "L0_gnn_bn_gamma": _L0_gnn_in["bn_gamma"],
        "L0_gnn_bn_beta": _L0_gnn_in["bn_beta"],
    }

def reference(x, adj, L0_gnn_router_w, L0_gnn_router_b, L0_gnn_expert_w, L0_gnn_bn_gamma, L0_gnn_bn_beta):
    import jax
    import jax.numpy as jnp
    def _L0_gnn_ref(x, adj, router_w, router_b, expert_w, bn_gamma, bn_beta):
        import jax, jax.numpy as jnp
        import numpy as np
        B, N, H, E = (64, 512, 1024, 4)
        BN_EPS = 1e-05
        scores = x.mean(axis=1) @ router_w + router_b
        top1 = jnp.argmax(scores, axis=-1)
        n_exp = expert_w.shape[0]
        W = expert_w[top1]
        support = jnp.einsum('bnh,bhk->bnk', x, W)
        out = jnp.einsum('bnm,bmk->bnk', adj, support)
        s = jax.ops.segment_sum(out.sum(axis=1), top1, num_segments=n_exp)
        ss = jax.ops.segment_sum((out * out).sum(axis=1), top1, num_segments=n_exp)
        cnt = jax.ops.segment_sum(jnp.ones_like(top1, dtype=out.dtype), top1, num_segments=n_exp) * out.shape[1]
        cnt = jnp.maximum(cnt, 1.0)[:, None]
        mean = s / cnt
        var = ss / cnt - mean * mean
        m = mean[top1][:, None, :]
        inv = jax.lax.rsqrt(var[top1][:, None, :] + BN_EPS)
        y = (out - m) * inv * bn_gamma[top1][:, None, :] + bn_beta[top1][:, None, :]
        return jax.nn.relu(y)

    x = _layernorm(x + _L0_gnn_ref(x, adj, L0_gnn_router_w, L0_gnn_router_b, L0_gnn_expert_w, L0_gnn_bn_gamma, L0_gnn_bn_beta), axis=-1)
    return x


_drawn_inputs = setup_inputs


def setup_inputs(seed=0):
    import zlib

    import numpy as np

    out = dict(_drawn_inputs(seed))
    spreads = {'L0_gnn_bn_gamma': (1.0, 0.2), 'L0_gnn_bn_beta': (0.0, 0.1)}
    factors = {}
    for name, (base, spread) in spreads.items():
        noise = np.random.default_rng([zlib.crc32(name.encode()), seed]).standard_normal(out[name].shape)
        drawn = base * np.exp(spread * noise) if base else spread * noise
        out[name] = jnp.asarray(drawn.astype(out[name].dtype))
    for name, factor in factors.items():
        out[name] = (out[name] * factor).astype(out[name].dtype)
    return out
```

```python
from contextlib import ExitStack

import concourse.bass as bass
from concourse import mybir

F32 = mybir.dt.float32
F32R = mybir.dt.float32r
U32 = mybir.dt.uint32
ALU = mybir.AluOpType
ACT = mybir.ActivationFunctionType
AX_X = mybir.AxisListType.X

P = 128
BANK = 512
BN_EPS = 1e-5
LN_EPS = 1e-5


def graph_layer(nc, x, adj, router_w, router_b, expert_w, bn_gamma, bn_beta, y):
    B, N, H = x.shape
    E = router_w.shape[1]
    K = expert_w.shape[2]
    C = H // P
    assert N == H == K and C == 8 and E == 4 and N == 2 * BANK
    STEPS = 2 * C
    PAIR = 2 * P
    PAIRS = C // 2
    PAIR_IN = 16 * 4
    QUAD = 4
    SCORES = 8
    GB = 2 * E * C

    QUADRANT = 32
    QUADS = P // QUADRANT
    adj_blocks = adj.rearrange("b (c i r) (j m) -> b c j r i m", i=QUADS, r=QUADRANT, j=QUADS)
    x_pairs = x.rearrange("b (j c r) (q h) -> b q j r c h", j=QUADS, r=QUADRANT, h=PAIR)
    w_pairs = expert_w.rearrange("e (c j r) (q k) -> e q j r c k", j=QUADS, r=QUADRANT, k=PAIR)
    outT = nc.dram_tensor("outT_scratch", (B, K, N), F32, kind="Internal").ap()
    outT_rows = outT.rearrange("b (c p) n -> b c p n", p=P)

    with ExitStack() as whole:
        def sem(name):
            return whole.enter_context(nc.semaphore(name))

        stats = whole.enter_context(nc.sbuf_tensor("stats", [P, B, C, 4, 3], F32))
        choice = whole.enter_context(nc.sbuf_tensor("choice", [1, B], F32))
        ones = whole.enter_context(nc.sbuf_tensor("ones", [P, P], F32))
        ident = whole.enter_context(nc.sbuf_tensor("ident", [P, P], F32))
        gb_rows = whole.enter_context(nc.sbuf_tensor("gb_rows", [GB, P], F32))
        carried = sem("carried")
        gb_in = sem("gb_in")

        with ExitStack() as ctx:
            def sb(name, shape, dt=F32):
                return ctx.enter_context(nc.sbuf_tensor(name, shape, dt))

            def psum(name, shape):
                return ctx.enter_context(nc.psum_tensor(name, shape, F32))

            adjT_hi, adjT_lo = sb("adjT_hi", [P, C, N], F32R), sb("adjT_lo", [P, C, N], F32R)
            zT_hi, zT_lo = sb("zT_hi", [P, C, N], F32R), sb("zT_lo", [P, C, N], F32R)
            raw = [sb(f"raw{i}", [P, C, PAIR]) for i in range(2)]
            st_hi = [sb(f"st_hi{i}", [P, C, P], F32R) for i in range(2)]
            st_lo = [sb(f"st_lo{i}", [P, C, P], F32R) for i in range(2)]
            adj_raw = [sb(f"adj_raw{i}", [P, QUADS, N // QUADS]) for i in range(2)]
            turned = [sb(f"turned{i}", [P, C, P]) for i in range(2)]
            out_sb = [sb(f"out_sb{i}", [P, N]) for i in range(2)]
            x_sums = sb("x_sums", [P, H])
            x_mean = sb("x_mean", [P, C])
            r_w = sb("r_w", [P, C, SCORES])
            r_b = sb("r_b", [1, SCORES])
            scores = sb("scores", [1, SCORES])
            best = sb("best", [1, 8])
            best_at = sb("best_at", [1, 8], U32)

            acc = [psum(f"acc{i}", [P, N]) for i in range(2)]
            p_router = psum("p_router", [P, BANK])

            ones_ready = sem("ones_ready")
            ident_ready = sem("ident_ready")
            router_in = sem("router_in")
            raw_in = [sem(f"raw_in{i}") for i in range(2)]
            adj_in = [sem(f"adj_in{i}") for i in range(2)]
            out_stored = [sem(f"out_stored{i}") for i in range(2)]
            st_hi_ready = sem("st_hi_ready")
            st_lo_ready = sem("st_lo_ready")
            products_done = sem("products_done")
            acc_free_act = sem("acc_free_act")
            acc_free_dve = sem("acc_free_dve")
            adj_turned = sem("adj_turned")
            adjT_hi_ready = sem("adjT_hi_ready")
            adjT_lo_ready = sem("adjT_lo_ready")
            out_copied = sem("out_copied")
            x_summed = sem("x_summed")
            x_totals = sem("x_totals")
            x_means = sem("x_means")
            scored = sem("scored")
            router_dve = sem("router_dve")
            chosen = sem("chosen")

            with nc.Block() as block:
                @block.sync
                def _(sp):
                    def load_quadrants(pair, src):
                        for j in range(QUADS):
                            sp.dma_start(raw[pair % 2][j * QUADRANT:(j + 1) * QUADRANT],
                                         src[j]).then_inc(raw_in[pair % 2], 16)

                    for q in range(2):
                        load_quadrants(q, x_pairs[0, q])

                    def load(pair, step, src):
                        sp.wait_ge(st_hi_ready, step - 2)
                        sp.wait_ge(st_lo_ready, step - 2)
                        load_quadrants(pair, src)

                    with sp.Fori(0, B) as b:
                        for q in range(2, PAIRS):
                            sp.wait_ge(x_summed, b * PAIRS + q - 1)
                            sp.sem_inc(carried, 1)
                            load(q, b * STEPS + 2 * q, x_pairs[b, q])
                        sp.wait_ge(chosen, b + 1)
                        sp.sem_inc(carried, 1)
                        e = sp.value_load(best_at[0:1, 0:1], min_val=0, max_val=E - 1)
                        for q in range(PAIRS):
                            load(q, b * STEPS + C + 2 * q, w_pairs[e, q])
                        for q in range(2):
                            load(q, b * STEPS + STEPS + 2 * q, x_pairs[(b + 1) % B, q])
                    for s in raw_in:
                        sp.wait_ge(s, PAIR_IN * (B * PAIRS + 1))

                @block.gpsimd
                def _(pool):
                    def load_adj(c, src):
                        for j in range(QUADS):
                            pool.dma_start(adj_raw[c % 2][j * QUADRANT:(j + 1) * QUADRANT],
                                           src[j]).then_inc(adj_in[c % 2], 16)

                    for c in range(2):
                        load_adj(c, adj_blocks[0, c])
                    pool.memset(ones[:], 1.0).then_inc(ones_ready, 1)
                    pool.memset(ident[:], 0.0).then_inc(ident_ready, 1)
                    pool.wait_ge(ident_ready, 1)
                    pool.affine_select(out=ident[:], in_=ident[:], compare_op=ALU.not_equal, fill=1.0, base=0,
                                       pattern=[[-1, P]], channel_multiplier=1).then_inc(ident_ready, 1)
                    for c in range(2, C):
                        pool.wait_ge(adj_turned, c - 1)
                        load_adj(c, adj_blocks[0, c])
                    with pool.Fori(0, B) as b:
                        for c in range(C):
                            pool.wait_ge(adj_turned, b * C + C + c - 1)
                            load_adj(c, adj_blocks[(b + 1) % B, c])

                @block.tensor
                def _(pe):
                    pe.wait_ge(ones_ready, 1)
                    pe.wait_ge(ident_ready, 2)

                    def products(step, c, mv_hi, mv_lo, before_last=None):
                        pe.wait_ge(st_hi_ready, step + 1)
                        pe.wait_ge(st_lo_ready, step + 1)
                        pe.wait_ge(acc_free_act, step + 1)
                        pe.wait_ge(acc_free_dve, step + 1)
                        for t in range(C):
                            if t == C - 1 and before_last:
                                before_last()
                            for n, (st, mv) in enumerate(((st_hi, mv_hi), (st_hi, mv_lo), (st_lo, mv_hi))):
                                for half in range(N // BANK):
                                    cols = slice(half * BANK, (half + 1) * BANK)
                                    last = pe.matmul(acc[c % 2][:, cols], st[c % 2][:, t, :], mv[:, t, cols],
                                                     start=(t == 0 and n == 0), stop=(t == C - 1 and n == 2))
                        last.then_inc(products_done, 1)

                    with pe.Fori(0, B) as b:
                        pe.wait_ge(adjT_hi_ready, b * C + C)
                        pe.wait_ge(adjT_lo_ready, b * C + C)
                        for c in range(C):
                            if c == 5:
                                pe.wait_ge(x_summed, b * PAIRS + PAIRS)
                                for h in range(C):
                                    last = pe.matmul(p_router[:, h:h + 1], x_sums[:, h * P:(h + 1) * P],
                                                     ones[:, 0:1], start=True, stop=True)
                                last.then_inc(x_totals, 1)
                            if c == 6:
                                pe.wait_ge(x_means, b + 1)
                                for h in range(C):
                                    last = pe.matmul(p_router[0:1, 64:64 + SCORES], x_mean[:, h:h + 1], r_w[:, h, :],
                                                     start=(h == 0), stop=(h == C - 1))
                                last.then_inc(scored, 1)
                            products(b * STEPS + c, c, adjT_hi, adjT_lo)

                        with pe.Fori(0, C // QUAD) as quad:
                            for j in range(QUAD):
                                step = b * STEPS + C + quad * QUAD + j

                                def last_z():
                                    pe.wait_ge(acc_free_act, step + 2)
                                    pe.wait_ge(acc_free_dve, step + 2)
                                products(step, j, zT_hi, zT_lo, before_last=last_z)

                def block_of(c):
                    return slice(c * P, (c + 1) * P)

                @block.scalar
                def _(act):
                    act.dma_start(r_w[:, :, 0:E], router_w.rearrange("(c p) e -> p c e", p=P)).then_inc(router_in, 16)
                    act.dma_start(r_b[:, 0:E], router_b.rearrange("(a e) -> a e", a=1)).then_inc(router_in, 16)
                    for n, table in enumerate((bn_gamma, bn_beta)):
                        act.dma_start(gb_rows[n * E * C:(n + 1) * E * C, :],
                                      table.rearrange("e (c p) -> (e c) p", p=P)).then_inc(gb_in, 16)
                    act.sem_inc(acc_free_act, 2)
                    for s in out_stored:
                        act.sem_inc(s, 16)

                    def split_adj(block_no, slot, cols):
                        act.wait_ge(adj_turned, block_no + 1)
                        act.activation(adjT_hi[:, :, cols], turned[slot][:], ACT.Copy).then_inc(adjT_hi_ready, 1)

                    def split_stationary(slot, half, uses):
                        if half == 0:
                            act.wait_ge(raw_in[slot], PAIR_IN * uses)
                        act.activation(st_hi[half][:], raw[slot][:, :, half * P:(half + 1) * P],
                                       ACT.Copy).then_inc(st_hi_ready, 1)

                    for c in range(C):
                        split_adj(c, c % 2, block_of(c))
                    for half in range(2):
                        split_stationary(0, half, 1)

                    with act.Fori(0, B) as b:
                        for c in range(C):
                            act.wait_ge(products_done, b * STEPS + c + 1)
                            act.activation(zT_hi[:, c, :], acc[c % 2][:], ACT.Copy).then_inc(acc_free_act, 1)
                            pair = c // 2 + 1
                            split_stationary(pair % 2, c % 2, b * PAIRS + pair // 2 + 1)
                        with act.Fori(0, C // QUAD) as quad:
                            for j in range(QUAD):
                                c = quad * QUAD + j
                                split_adj(b * C + C + c, j % 2, bass.ds(c * P, P))
                                act.wait_ge(out_stored[j % 2], (b * (C // 2) + quad * (QUAD // 2) + j // 2 + 1) * 16)
                                act.wait_ge(products_done, b * STEPS + C + c + 1)
                                act.activation(out_sb[j % 2][:], acc[j % 2][:], ACT.Copy).then_inc(acc_free_act, 1)
                                pair = j // 2 + 1
                                split_stationary(pair % 2, j % 2, b * PAIRS + PAIRS // 2 + quad + pair // 2 + 1)
                                act.wait_ge(acc_free_act, b * STEPS + C + c + 3)
                                act.dma_start(outT_rows[b, c], out_sb[j % 2][:]).then_inc(out_stored[j % 2], 16)
                    for s in out_stored:
                        act.wait_ge(s, 16 * (B * C // 2 + 1))

                @block.vector
                def _(dve):
                    dve.sem_inc(acc_free_dve, 2)
                    dve.wait_ge(router_in, 32)
                    for e in range(E, SCORES):
                        dve.tensor_copy(r_w[:, :, e:e + 1], r_w[:, :, E - 1:E])
                        dve.tensor_copy(r_b[:, e:e + 1], r_b[:, E - 1:E])

                    def turn_adj(slot, uses, split_before=None):
                        if split_before is not None:
                            dve.wait_ge(adjT_lo_ready, split_before)
                        dve.wait_ge(adj_in[slot], PAIR_IN * uses)
                        dve.transpose(turned[slot][:].rearrange("p c (i r) -> p c i r", r=QUADRANT),
                                      adj_raw[slot][:].rearrange("p i (c r) -> p c i r", r=QUADRANT)
                                      ).then_inc(adj_turned, 1)

                    def split_adj(block_no, slot, cols):
                        dve.wait_ge(adjT_hi_ready, block_no + 1)
                        dve.tensor_tensor(adjT_lo[:, :, cols], turned[slot][:], adjT_hi[:, :, cols].bitcast(F32),
                                          ALU.subtract).then_inc(adjT_lo_ready, 1)

                    def split_stationary(slot, half, step):
                        dve.wait_ge(st_hi_ready, step + 1)
                        dve.tensor_tensor(st_lo[half][:], raw[slot][:, :, half * P:(half + 1) * P],
                                          st_hi[half][:].bitcast(F32), ALU.subtract).then_inc(st_lo_ready, 1)

                    def sum_pair(pair, uses):
                        dve.wait_ge(raw_in[pair % 2], PAIR_IN * uses)
                        dve.tensor_reduce(x_sums[:, pair * PAIR:(pair + 1) * PAIR],
                                          raw[pair % 2][:].rearrange("p c h -> p h c"), AX_X,
                                          ALU.add).then_inc(x_summed, 1)

                    turn_adj(0, 1)
                    for c in range(C):
                        if c + 1 < C:
                            turn_adj((c + 1) % 2, (c + 1) // 2 + 1, c if c else None)
                        split_adj(c, c % 2, block_of(c))
                    for half in range(2):
                        split_stationary(0, half, half)
                    for pair in range(2):
                        sum_pair(pair, 1)

                    with dve.Fori(0, B) as b:
                        for c in range(C):
                            dve.wait_ge(acc_free_act, b * STEPS + c + 3)
                            dve.tensor_tensor(zT_lo[:, c, :], acc[c % 2][:], zT_hi[:, c, :].bitcast(F32),
                                              ALU.subtract).then_inc(acc_free_dve, 1)
                            split_stationary((c // 2 + 1) % 2, c % 2, b * STEPS + c + 2)
                            if c in (1, 3):
                                sum_pair(c // 2 + 2, b * PAIRS + 2)
                            if c == 4:
                                dve.wait_ge(x_totals, b + 1)
                                dve.tensor_scalar(x_mean[:], p_router[:, 0:C], 1.0 / N, None,
                                                  ALU.mult).then_inc(x_means, 1)
                            if c == 5:
                                dve.wait_ge(scored, b + 1)
                                dve.tensor_tensor(scores[:], p_router[0:1, 64:64 + SCORES], r_b[:],
                                                  ALU.add).then_inc(router_dve, 1)
                                dve.wait_ge(router_dve, 2 * b + 1)
                                dve.sem_inc(carried, 1)
                                dve.max(best[:], scores[:]).then_inc(router_dve, 1)
                                dve.wait_ge(router_dve, 2 * b + 2)
                                dve.sem_inc(carried, 1)
                                dve.max_index(best_at[:], best[:], scores[:]).then_inc(chosen, 1)
                                dve.wait_ge(chosen, b + 1)
                                dve.tensor_copy(choice[0:1, bass.ds(b, 1)], best_at[0:1, 0:1])
                        with dve.Fori(0, C // QUAD) as quad:
                            for j in range(QUAD):
                                c = quad * QUAD + j
                                turn_adj(j % 2, b * (C // 2) + C // 2 + quad * (QUAD // 2) + j // 2 + 1,
                                         b * C + C + c - 1)
                                split_adj(b * C + C + c, j % 2, bass.ds(c * P, P))
                                dve.wait_ge(acc_free_act, b * STEPS + C + c + 3)
                                for half in range(N // BANK):
                                    last = dve.bn_stats(
                                        stats[:, b, c, 2 * half:2 * half + 2, :].rearrange("p g s -> p (g s)"),
                                        acc[j % 2][:, half * BANK:(half + 1) * BANK])
                                last.then_inc(acc_free_dve, 1)
                                split_stationary((j // 2 + 1) % 2, j % 2, b * STEPS + C + c + 2)
                        for pair in range(2):
                            sum_pair(pair, b * PAIRS + PAIRS + 1)

        ROWS = BANK
        TILES = ROWS // P
        UNITS = B * N // ROWS
        PER_GRAPH = N // ROWS
        SLOTS = 4
        GROUP = N // 4

        outT_units = outT.rearrange("b (c p) (u n) -> b u p c n", p=P, n=ROWS)
        x_units = x.rearrange("b (u t p) h -> (b u) p t h", t=TILES, p=P)
        y_units = y.rearrange("b (u t p) h -> (b u) p t h", t=TILES, p=P)

        with ExitStack() as ctx:
            def sb(name, shape, dt=F32):
                return ctx.enter_context(nc.sbuf_tensor(name, shape, dt))

            out_u = [sb(f"out_u{i}", [P, C, ROWS]) for i in range(SLOTS)]
            x_u = [sb(f"x_u{i}", [P, TILES, H]) for i in range(SLOTS)]
            tile_ps = [ctx.enter_context(nc.psum_tensor(f"tile_ps{i}", [P, K], F32)) for i in range(TILES)]
            choice_all = sb("choice_all", [P, B])
            is_expert = sb("is_expert", [P, E, B])
            per_count = sb("per_count", [P, E])
            squares = sb("squares", [P, B, C, 4])
            sum_1, sum_2 = sb("sum_1", [P, B, C]), sb("sum_2", [P, B, C])
            masked = sb("masked", [P, E * B * C])
            mean, var = sb("mean", [P, E, C]), sb("var", [P, E, C])
            mean_sq = sb("mean_sq", [P, E, C])
            gamma_beta = sb("gamma_beta", [P, 2, E, C])
            scale, shift = sb("scale", [P, B, C]), sb("shift", [P, B, C])
            ln_stats = sb("ln_stats", [P, TILES, 2, 6])
            ln_var_eps = sb("ln_var_eps", [P, TILES])
            minus_half = sb("minus_half", [P, E, C])
            ln_mv = sb("ln_mv", [P, TILES, 2])
            ln_scale = [sb(f"ln_scale{i}", [P, TILES]) for i in range(SLOTS)]
            ln_shift = [sb(f"ln_shift{i}", [P, TILES]) for i in range(SLOTS)]

            out_in = [sem(f"out_in{i}") for i in range(SLOTS)]
            x_in = [sem(f"x_in{i}") for i in range(SLOTS)]
            y_stored = [sem(f"y_stored{i}") for i in range(SLOTS)]
            tables_in_ps = sem("tables_in_ps")
            bn_steps = sem("bn_steps")
            bn_ready = sem("bn_ready")
            relu_done = sem("relu_done")
            tile_turned = sem("tile_turned")
            tile_added = sem("tile_added")
            ln_taken = sem("ln_taken")
            half_ready = sem("half_ready")
            ln_aggregated = sem("ln_aggregated")
            bn_var = sem("bn_var")
            bn_inverse = sem("bn_inverse")
            ln_var = sem("ln_var")
            ln_inverse = sem("ln_inverse")
            ln_ready = sem("ln_ready")
            y_ready = sem("y_ready")

            with nc.Block() as block:
                @block.sync
                def _(sp):
                    def load(u_out, u_x, slot):
                        sp.dma_start(out_u[slot][:], u_out).then_inc(out_in[slot], 16)
                        sp.dma_start(x_u[slot][:], u_x).then_inc(x_in[slot], 16)

                    for slot in range(SLOTS):
                        load(outT_units[slot // PER_GRAPH, slot % PER_GRAPH], x_units[slot], slot)
                    with sp.Fori(0, UNITS // SLOTS - 1) as i:
                        for slot in range(SLOTS):
                            graph = (i + 1) * (SLOTS // PER_GRAPH) + slot // PER_GRAPH
                            sp.wait_ge(tile_turned, (i * SLOTS + slot + 1) * TILES)
                            sp.wait_ge(y_stored[slot], (i + 1) * 16)
                            load(outT_units[graph, slot % PER_GRAPH], x_units[(i + 1) * SLOTS + slot], slot)

                @block.gpsimd
                def _(pool):
                    pool.memset(minus_half[:], -0.5).then_inc(half_ready, 1)
                    pool.wait_ge(half_ready, 1)
                    pool.wait_ge(bn_var, 1)
                    pool.tensor_tensor(var[:], var[:], minus_half[:], ALU.pow).then_inc(bn_inverse, 1)
                    with pool.Fori(0, UNITS // SLOTS) as i:
                        for slot in range(SLOTS):
                            pool.wait_ge(ln_var, i * SLOTS + slot + 1)
                            pool.tensor_tensor(ln_scale[slot][:], ln_var_eps[:], minus_half[:, 0, 0:TILES],
                                               ALU.pow).then_inc(ln_inverse, 1)

                @block.tensor
                def _(pe):
                    pe.matmul(tile_ps[3][:, 0:B], ones[0:1, :], choice[:], start=True, stop=True).then_inc(tables_in_ps, 1)
                    pe.wait_ge(gb_in, 32)
                    pe.transpose(tile_ps[3][:, BANK:BANK + GB], gb_rows[:], ident[0:GB, 0:GB]).then_inc(tables_in_ps, 1)
                    pe.wait_ge(bn_ready, 1)
                    with pe.Fori(0, UNITS // SLOTS) as i:
                        for slot in range(SLOTS):
                            pe.wait_ge(relu_done, i * SLOTS + slot + 1)
                            for t in range(TILES):
                                pe.wait_ge(tile_added, (i * SLOTS + slot) * TILES + t + 1)
                                for c in range(C):
                                    last = pe.transpose(tile_ps[t][:, c * P:(c + 1) * P],
                                                        out_u[slot][:, c, t * P:(t + 1) * P], ident[:])
                                last.then_inc(tile_turned, 1)

                @block.scalar
                def _(act):
                    act.wait_ge(bn_ready, 1)

                    def relu(graph, slot, uses):
                        act.wait_ge(out_in[slot], 16 * uses)
                        act.sem_inc(carried, 1)
                        for c in range(C):
                            last = act.activation(out_u[slot][:, c, :], out_u[slot][:, c, :], ACT.Relu,
                                                  bias=shift[:, graph, c:c + 1], scale=scale[:, graph, c:c + 1])
                        last.then_inc(relu_done, 1)

                    def normalise_and_store(unit, slot):
                        act.wait_ge(ln_ready, unit + 1)
                        for t in range(TILES):
                            last = act.activation(x_u[slot][:, t, :], x_u[slot][:, t, :], ACT.Identity,
                                                  bias=ln_shift[slot][:, t:t + 1], scale=ln_scale[slot][:, t:t + 1])
                        last.then_inc(y_ready, 1)
                        act.wait_ge(y_ready, unit + 1)
                        act.dma_start(y_units[unit], x_u[slot][:]).then_inc(y_stored[slot], 16)

                    relu(0, 0, 1)
                    with act.Fori(0, UNITS // SLOTS - 1) as i:
                        for slot in range(SLOTS):
                            ahead = slot + 1
                            relu(i * (SLOTS // PER_GRAPH) + ahead // PER_GRAPH, ahead % SLOTS, i + ahead // SLOTS + 1)
                            normalise_and_store(i * SLOTS + slot, slot)
                    for unit in range(UNITS - SLOTS, UNITS):
                        ahead = unit + 1
                        if ahead < UNITS:
                            relu(ahead // PER_GRAPH, ahead % SLOTS, ahead // SLOTS + 1)
                        normalise_and_store(unit, unit % SLOTS)
                    for s in y_stored:
                        act.wait_ge(s, 16 * (UNITS // SLOTS))

                @block.vector
                def _(dve):
                    done = [0]

                    def then(instruction):
                        done[0] += 1
                        instruction.then_inc(bn_steps, 1)
                        dve.wait_ge(bn_steps, done[0])

                    means, sq_devs = stats[:, :, :, :, 1], stats[:, :, :, :, 2]

                    dve.tensor_reduce(sum_1[:], means, AX_X, ALU.add)
                    then(dve.tensor_tensor(squares[:], means, means, ALU.mult))
                    then(dve.scalar_tensor_tensor(out=squares[:], in0=squares[:], scalar=float(GROUP), in1=sq_devs,
                                                  op0=ALU.mult, op1=ALU.add))
                    then(dve.tensor_reduce(sum_2[:], squares[:], AX_X, ALU.add))
                    dve.wait_ge(tables_in_ps, 1)
                    then(dve.tensor_copy(choice_all[:], tile_ps[3][:, 0:B]))
                    for e in range(E):
                        last = dve.tensor_scalar(is_expert[:, e, :], choice_all[:], float(e), None, ALU.is_equal)
                    then(last)
                    then(dve.tensor_reduce(per_count[:], is_expert[:], AX_X, ALU.add))
                    then(dve.tensor_scalar(per_count[:], per_count[:], float(N), 1.0, ALU.mult, ALU.max))
                    then(dve.reciprocal(per_count[:], per_count[:]))
                    by_expert = masked[:].rearrange("p (e b c) -> p e b c", e=E, b=B)
                    of_graph = is_expert[:].unsqueeze(3).to_broadcast([P, E, B, C])
                    count_of = per_count[:].unsqueeze(2).to_broadcast([P, E, C])
                    for total, moment, unit in ((sum_1, mean, float(GROUP)), (sum_2, var, 1.0)):
                        then(dve.tensor_tensor(by_expert, total[:].unsqueeze(1).to_broadcast([P, E, B, C]),
                                               of_graph, ALU.mult))
                        then(dve.tensor_reduce(moment[:], by_expert.rearrange("p e b c -> p e c b"), AX_X, ALU.add))
                        then(dve.scalar_tensor_tensor(out=moment[:], in0=moment[:], scalar=unit, in1=count_of,
                                                      op0=ALU.mult, op1=ALU.mult))
                    then(dve.tensor_tensor(mean_sq[:], mean[:], mean[:], ALU.mult))
                    then(dve.tensor_tensor(var[:], var[:], mean_sq[:], ALU.subtract))
                    dve.tensor_scalar(var[:], var[:], BN_EPS, None, ALU.add).then_inc(bn_var, 1)
                    dve.wait_ge(bn_inverse, 1)
                    dve.wait_ge(tables_in_ps, 2)
                    then(dve.tensor_copy(gamma_beta[:].rearrange("p g e c -> p (g e c)"),
                                         tile_ps[3][:, BANK:BANK + GB]))
                    then(dve.tensor_tensor(var[:], var[:], gamma_beta[:, 0], ALU.mult))
                    then(dve.tensor_tensor(mean[:], mean[:], var[:], ALU.mult))
                    then(dve.tensor_tensor(mean[:], gamma_beta[:, 1], mean[:], ALU.subtract))
                    by_graph = masked[:].rearrange("p (b c e) -> p b c e", e=E, b=B)
                    expert_of = is_expert[:].rearrange("p e b -> p b e").unsqueeze(2).to_broadcast([P, B, C, E])
                    for table, own in ((var, scale), (mean, shift)):
                        then(dve.tensor_tensor(by_graph, expert_of,
                                               table[:].rearrange("p e c -> p c e").unsqueeze(1).to_broadcast([P, B, C, E]),
                                               ALU.mult))
                        then(dve.tensor_reduce(own[:], by_graph, AX_X, ALU.add))
                    dve.sem_inc(tile_added, TILES)
                    dve.sem_inc(bn_ready, 1)

                    with dve.Fori(0, UNITS // SLOTS) as i:
                        for slot in range(SLOTS):
                            unit = i * SLOTS + slot
                            dve.wait_ge(x_in[slot], (i + 1) * 16)
                            for t in range(TILES):
                                dve.wait_ge(tile_turned, unit * TILES + t + 1)
                                dve.tensor_tensor(x_u[slot][:, t, :], x_u[slot][:, t, :], tile_ps[t][:],
                                                  ALU.add).then_inc(tile_added, 1)
                                dve.wait_ge(tile_added, unit * TILES + TILES + t + 1)
                                for half in range(H // BANK):
                                    last = dve.bn_stats(ln_stats[:, t, half, :],
                                                        x_u[slot][:, t, half * BANK:(half + 1) * BANK])
                                last.then_inc(ln_taken, 1)
                            dve.wait_ge(ln_taken, unit * TILES + TILES)
                            dve.sem_inc(carried, 1)
                            for t in range(TILES):
                                last = dve.bn_aggr(ln_mv[:, t, :], ln_stats[:, t].rearrange("p a s -> p (a s)"))
                            last.then_inc(ln_aggregated, 1)
                            dve.wait_ge(ln_aggregated, unit + 1)
                            dve.tensor_scalar(ln_var_eps[:], ln_mv[:, :, 1], LN_EPS, None,
                                              ALU.add).then_inc(ln_var, 1)
                            dve.wait_ge(ln_inverse, unit + 1)
                            dve.scalar_tensor_tensor(out=ln_shift[slot][:], in0=ln_mv[:, :, 0], scalar=-1.0,
                                                     in1=ln_scale[slot][:], op0=ALU.mult,
                                                     op1=ALU.mult).then_inc(ln_ready, 1)


INPUTS = ["x", "adj", "L0_gnn_router_w", "L0_gnn_router_b", "L0_gnn_expert_w", "L0_gnn_bn_gamma", "L0_gnn_bn_beta"]


def kernel(**inputs):
    import numpy as np
    import concourse.bacc as bacc
    from concourse.bass_utils import run_bass_kernel_spmd

    nc = bacc.Bacc("TRN2", target_bir_lowering=False, num_devices=1)
    arrays, args = {}, []
    for name in INPUTS:
        a = np.ascontiguousarray(inputs[name])
        arrays[f"in_{name}"] = a
        args.append(nc.dram_tensor(f"in_{name}", a.shape, mybir.dt.from_np(a.dtype), kind="ExternalInput").ap())
    y = nc.dram_tensor("out_y", inputs["x"].shape, F32, kind="ExternalOutput").ap()
    graph_layer(nc, *args, y)
    return run_bass_kernel_spmd(nc, [arrays], core_ids=[0]).results[0]["out_y"]
```

```python
from contextlib import ExitStack

import concourse.bass as bass
from concourse import mybir

F32 = mybir.dt.float32
F32R = mybir.dt.float32r
U32 = mybir.dt.uint32
ALU = mybir.AluOpType
ACT = mybir.ActivationFunctionType
AX_X = mybir.AxisListType.X

P = 128
BANK = 512
BN_EPS = 1e-5
LN_EPS = 1e-5


def graph_layer(nc, x, adj, router_w, router_b, expert_w, bn_gamma, bn_beta, y):
    B, N, H = x.shape
    E = router_w.shape[1]
    K = expert_w.shape[2]
    C = H // P
    assert N == H == K and C == 8 and E == 4 and N == 2 * BANK
    STEPS = 2 * C
    PAIR = 2 * P
    PAIRS = C // 2
    PAIR_IN = 16 * 4
    QUAD = 4
    SCORES = 8
    GB = 2 * E * C

    QUADRANT = 32
    QUADS = P // QUADRANT
    adj_blocks = adj.rearrange("b (c i r) (j m) -> b c j r i m", i=QUADS, r=QUADRANT, j=QUADS)
    x_pairs = x.rearrange("b (j c r) (q h) -> b q j r c h", j=QUADS, r=QUADRANT, h=PAIR)
    w_pairs = expert_w.rearrange("e (c j r) (q k) -> e q j r c k", j=QUADS, r=QUADRANT, k=PAIR)
    outT = nc.dram_tensor("outT_scratch", (B, K, N), F32, kind="Internal").ap()
    outT_rows = outT.rearrange("b (c p) n -> b c p n", p=P)

    with ExitStack() as whole:
        def sem(name):
            return whole.enter_context(nc.semaphore(name))

        stats = whole.enter_context(nc.sbuf_tensor("stats", [P, B, C, 4, 3], F32))
        choice = whole.enter_context(nc.sbuf_tensor("choice", [1, B], F32))
        ones = whole.enter_context(nc.sbuf_tensor("ones", [P, P], F32))
        ident = whole.enter_context(nc.sbuf_tensor("ident", [P, P], F32))
        gb_rows = whole.enter_context(nc.sbuf_tensor("gb_rows", [GB, P], F32))
        carried = sem("carried")
        gb_in = sem("gb_in")

        ROWS = 2 * P
        TILES = ROWS // P
        UNITS = B * N // ROWS
        PER_GRAPH = N // ROWS
        SLOTS = 8
        EARLY = 4

        outT_units = outT.rearrange("b (c p) (u n) -> b u p c n", p=P, n=ROWS)
        x_units = x.rearrange("b (u t p) h -> (b u) p t h", t=TILES, p=P)
        y_units = y.rearrange("b (u t p) h -> (b u) p t h", t=TILES, p=P)

        at = nc.sbuf_base
        KEPT = C * N * 4
        UNIT = C * ROWS * 4
        whole.enter_context(nc.sbuf_tensor("adjT_or_units", [P, 2 * C * N], F32))
        adjT_hi = nc.alloc_sbuf_tensor_at("adjT_hi", [P, C, N], F32R, offset=at)
        adjT_lo = nc.alloc_sbuf_tensor_at("adjT_lo", [P, C, N], F32R, offset=at + KEPT)
        out_u = [nc.alloc_sbuf_tensor_at(f"out_u{i}", [P, C, ROWS], F32, offset=at + 2 * i * UNIT)
                 for i in range(EARLY)]
        x_u = [nc.alloc_sbuf_tensor_at(f"x_u{i}", [P, TILES, H], F32, offset=at + (2 * i + 1) * UNIT)
               for i in range(EARLY)]
        out_in = [sem(f"out_in{i}") for i in range(SLOTS)]
        x_in = [sem(f"x_in{i}") for i in range(SLOTS)]

        def load_unit(sp, graph, part, unit, slot):
            sp.dma_start(out_u[slot][:], outT_units[graph, part]).then_inc(out_in[slot], 16)
            sp.dma_start(x_u[slot][:], x_units[unit]).then_inc(x_in[slot], 16)

        with ExitStack() as ctx:
            def sb(name, shape, dt=F32):
                return ctx.enter_context(nc.sbuf_tensor(name, shape, dt))

            def psum(name, shape):
                return ctx.enter_context(nc.psum_tensor(name, shape, F32))

            zT_hi, zT_lo = sb("zT_hi", [P, C, N], F32R), sb("zT_lo", [P, C, N], F32R)
            raw = [sb(f"raw{i}", [P, C, PAIR]) for i in range(2)]
            st_hi = [sb(f"st_hi{i}", [P, C, P], F32R) for i in range(2)]
            st_lo = [sb(f"st_lo{i}", [P, C, P], F32R) for i in range(2)]
            adj_raw = [sb(f"adj_raw{i}", [P, QUADS, N // QUADS]) for i in range(QUAD)]
            turned = [sb(f"turned{i}", [P, C, P]) for i in range(2)]
            out_sb = [sb(f"out_sb{i}", [P, N]) for i in range(2)]
            x_sums = sb("x_sums", [P, H])
            x_mean = sb("x_mean", [P, C])
            r_w = sb("r_w", [P, C, SCORES])
            r_b = sb("r_b", [1, SCORES])
            scores = sb("scores", [1, SCORES])
            best = sb("best", [1, 8])
            best_at = sb("best_at", [1, 8], U32)

            acc = [psum(f"acc{i}", [P, N]) for i in range(2)]
            p_router = psum("p_router", [P, BANK])

            ones_ready = sem("ones_ready")
            ident_ready = sem("ident_ready")
            router_in = sem("router_in")
            raw_in = [sem(f"raw_in{i}") for i in range(2)]
            adj_in = [sem(f"adj_in{i}") for i in range(QUAD)]
            adj_first_in = [sem(f"adj_first_in{i}") for i in range(QUAD)]
            out_stored = [sem(f"out_stored{i}") for i in range(2)]
            st_hi_ready = sem("st_hi_ready")
            st_lo_ready = sem("st_lo_ready")
            products_done = sem("products_done")
            acc_free_act = sem("acc_free_act")
            acc_free_dve = sem("acc_free_dve")
            adj_turned = sem("adj_turned")
            adjT_hi_ready = sem("adjT_hi_ready")
            adjT_lo_ready = sem("adjT_lo_ready")
            out_copied = sem("out_copied")
            x_summed = sem("x_summed")
            x_totals = sem("x_totals")
            x_means = sem("x_means")
            scored = sem("scored")
            router_dve = sem("router_dve")
            chosen = sem("chosen")

            with nc.Block() as block:
                @block.sync
                def _(sp):
                    def load_quadrants(tile, src, landed):
                        for j in range(QUADS):
                            sp.dma_start(tile[j * QUADRANT:(j + 1) * QUADRANT], src[j]).then_inc(landed, 16)

                    for c in range(QUAD):
                        load_quadrants(adj_raw[c], adj_blocks[0, c], adj_first_in[c])
                        if c % 2:
                            load_quadrants(raw[c // 2], x_pairs[0, c // 2], raw_in[c // 2])

                    def load(pair, step, src):
                        sp.wait_ge(st_hi_ready, step - 2)
                        sp.wait_ge(st_lo_ready, step - 2)
                        load_quadrants(raw[pair % 2], src, raw_in[pair % 2])

                    def load_graph(b):
                        for q in range(2, PAIRS):
                            sp.wait_ge(x_summed, b * PAIRS + q - 1)
                            sp.sem_inc(carried, 1)
                            load(q, b * STEPS + 2 * q, x_pairs[b, q])
                        sp.wait_ge(chosen, b + 1)
                        sp.sem_inc(carried, 1)
                        e = sp.value_load(best_at[0:1, 0:1], min_val=0, max_val=E - 1)
                        for q in range(PAIRS):
                            load(q, b * STEPS + C + 2 * q, w_pairs[e, q])

                    with sp.Fori(0, B - 1) as b:
                        load_graph(b)
                        for q in range(2):
                            load(q, b * STEPS + STEPS + 2 * q, x_pairs[b + 1, q])
                    load_graph(B - 1)

                    sp.wait_ge(products_done, (B - 1) * STEPS + C)
                    for s in out_stored:
                        sp.wait_ge(s, 16 * (C // 2 + 1))
                    for slot in range(EARLY):
                        load_unit(sp, slot // PER_GRAPH, slot % PER_GRAPH, slot, slot)

                @block.gpsimd
                def _(pool):
                    pool.memset(ones[:], 1.0).then_inc(ones_ready, 1)
                    pool.memset(ident[:], 0.0).then_inc(ident_ready, 1)
                    pool.wait_ge(ident_ready, 1)
                    pool.affine_select(out=ident[:], in_=ident[:], compare_op=ALU.not_equal, fill=1.0, base=0,
                                       pattern=[[-1, P]], channel_multiplier=1).then_inc(ident_ready, 1)

                    def load_adj(block_no, slot, src):
                        pool.wait_ge(adj_turned, block_no - QUAD + 1)
                        for j in range(QUADS):
                            pool.dma_start(adj_raw[slot][j * QUADRANT:(j + 1) * QUADRANT],
                                           src[j]).then_inc(adj_in[slot], 16)

                    for c in range(QUAD, C):
                        load_adj(c, c - QUAD, adj_blocks[0, c])
                    with pool.Fori(1, B) as b:
                        for c in range(C):
                            load_adj(b * C + c, c % QUAD, adj_blocks[b, c])

                @block.tensor
                def _(pe):
                    pe.wait_ge(ones_ready, 1)
                    pe.wait_ge(ident_ready, 2)

                    def products(step, c, mv_hi, mv_lo, before_last=None):
                        pe.wait_ge(st_hi_ready, step + 1)
                        pe.wait_ge(st_lo_ready, step + 1)
                        pe.wait_ge(acc_free_act, step + 1)
                        pe.wait_ge(acc_free_dve, step + 1)
                        for t in range(C):
                            if t == C - 1 and before_last:
                                before_last()
                            for n, (st, mv) in enumerate(((st_hi, mv_hi), (st_hi, mv_lo), (st_lo, mv_hi))):
                                for half in range(N // BANK):
                                    cols = slice(half * BANK, (half + 1) * BANK)
                                    last = pe.matmul(acc[c % 2][:, cols], st[c % 2][:, t, :], mv[:, t, cols],
                                                     start=(t == 0 and n == 0), stop=(t == C - 1 and n == 2))
                        last.then_inc(products_done, 1)

                    with pe.Fori(0, B) as b:
                        pe.wait_ge(adjT_hi_ready, b * C + C)
                        pe.wait_ge(adjT_lo_ready, b * C + C)
                        for c in range(C):
                            if c == 5:
                                pe.wait_ge(x_summed, b * PAIRS + PAIRS)
                                for h in range(C):
                                    last = pe.matmul(p_router[:, h:h + 1], x_sums[:, h * P:(h + 1) * P],
                                                     ones[:, 0:1], start=True, stop=True)
                                last.then_inc(x_totals, 1)
                            if c == 6:
                                pe.wait_ge(x_means, b + 1)
                                for h in range(C):
                                    last = pe.matmul(p_router[0:1, 64:64 + SCORES], x_mean[:, h:h + 1], r_w[:, h, :],
                                                     start=(h == 0), stop=(h == C - 1))
                                last.then_inc(scored, 1)
                            products(b * STEPS + c, c, adjT_hi, adjT_lo)

                        with pe.Fori(0, C // QUAD) as quad:
                            for j in range(QUAD):
                                step = b * STEPS + C + quad * QUAD + j

                                def last_z():
                                    pe.wait_ge(acc_free_act, step + 2)
                                    pe.wait_ge(acc_free_dve, step + 2)
                                products(step, j, zT_hi, zT_lo, before_last=last_z)

                def block_of(c):
                    return slice(c * P, (c + 1) * P)

                @block.scalar
                def _(act):
                    act.dma_start(r_w[:, :, 0:E], router_w.rearrange("(c p) e -> p c e", p=P)).then_inc(router_in, 16)
                    act.dma_start(r_b[:, 0:E], router_b.rearrange("(a e) -> a e", a=1)).then_inc(router_in, 16)
                    for n, table in enumerate((bn_gamma, bn_beta)):
                        act.dma_start(gb_rows[n * E * C:(n + 1) * E * C, :],
                                      table.rearrange("e (c p) -> (e c) p", p=P)).then_inc(gb_in, 16)
                    act.sem_inc(acc_free_act, 2)
                    for s in out_stored:
                        act.sem_inc(s, 16)

                    def split_adj(block_no, slot, cols):
                        act.wait_ge(adj_turned, block_no + 1)
                        act.activation(adjT_hi[:, :, cols], turned[slot][:], ACT.Copy).then_inc(adjT_hi_ready, 1)

                    def split_stationary(slot, half, uses):
                        if half == 0:
                            act.wait_ge(raw_in[slot], PAIR_IN * uses)
                        act.activation(st_hi[half][:], raw[slot][:, :, half * P:(half + 1) * P],
                                       ACT.Copy).then_inc(st_hi_ready, 1)

                    for c in range(C):
                        split_adj(c, c % 2, block_of(c))
                        if c in (C - 4, C - 3):
                            split_stationary(0, c - C + 4, 1)

                    def z_chunks(b):
                        for c in range(C):
                            act.wait_ge(products_done, b * STEPS + c + 1)
                            act.activation(zT_hi[:, c, :], acc[c % 2][:], ACT.Copy).then_inc(acc_free_act, 1)
                            pair = c // 2 + 1
                            split_stationary(pair % 2, c % 2, b * PAIRS + pair // 2 + 1)

                    def out_chunk(b, quad, j, split_next=True, adj_next=True):
                        c = quad * QUAD + j
                        if adj_next:
                            split_adj(b * C + C + c, j % 2, bass.ds(c * P, P))
                        act.wait_ge(out_stored[j % 2], (b * (C // 2) + quad * (QUAD // 2) + j // 2 + 1) * 16)
                        act.wait_ge(products_done, b * STEPS + C + c + 1)
                        act.activation(out_sb[j % 2][:], acc[j % 2][:], ACT.Copy).then_inc(acc_free_act, 1)
                        if split_next:
                            pair = j // 2 + 1
                            split_stationary(pair % 2, j % 2, b * PAIRS + PAIRS // 2 + quad + pair // 2 + 1)
                        act.wait_ge(acc_free_act, b * STEPS + C + c + 3)
                        act.dma_start(outT_rows[b, c], out_sb[j % 2][:]).then_inc(out_stored[j % 2], 16)

                    with act.Fori(0, B - 1) as b:
                        z_chunks(b)
                        with act.Fori(0, C // QUAD) as quad:
                            for j in range(QUAD):
                                out_chunk(b, quad, j)
                    z_chunks(B - 1)
                    for c in range(C):
                        out_chunk(B - 1, c // QUAD, c % QUAD, split_next=c < C - 2, adj_next=False)
                    for s in out_stored:
                        act.wait_ge(s, 16 * (B * C // 2 + 1))

                @block.vector
                def _(dve):
                    dve.sem_inc(acc_free_dve, 2)
                    dve.wait_ge(router_in, 32)
                    for e in range(E, SCORES):
                        dve.tensor_copy(r_w[:, :, e:e + 1], r_w[:, :, E - 1:E])
                        dve.tensor_copy(r_b[:, e:e + 1], r_b[:, E - 1:E])

                    def turn_adj(slot, landed, uses, split_before=None):
                        if split_before is not None:
                            dve.wait_ge(adjT_lo_ready, split_before)
                        dve.wait_ge(landed[slot], PAIR_IN * uses)
                        dve.transpose(turned[slot % 2][:].rearrange("p c (i r) -> p c i r", r=QUADRANT),
                                      adj_raw[slot][:].rearrange("p i (c r) -> p c i r", r=QUADRANT)
                                      ).then_inc(adj_turned, 1)

                    def split_adj(block_no, slot, cols):
                        dve.wait_ge(adjT_hi_ready, block_no + 1)
                        dve.tensor_tensor(adjT_lo[:, :, cols], turned[slot][:], adjT_hi[:, :, cols].bitcast(F32),
                                          ALU.subtract).then_inc(adjT_lo_ready, 1)

                    def split_stationary(slot, half, step):
                        dve.wait_ge(st_hi_ready, step + 1)
                        dve.tensor_tensor(st_lo[half][:], raw[slot][:, :, half * P:(half + 1) * P],
                                          st_hi[half][:].bitcast(F32), ALU.subtract).then_inc(st_lo_ready, 1)

                    def sum_pair(pair, uses):
                        dve.wait_ge(raw_in[pair % 2], PAIR_IN * uses)
                        dve.tensor_reduce(x_sums[:, pair * PAIR:(pair + 1) * PAIR],
                                          raw[pair % 2][:].rearrange("p c h -> p h c"), AX_X,
                                          ALU.add).then_inc(x_summed, 1)

                    turn_adj(0, adj_first_in, 1)
                    for c in range(C):
                        if c + 1 < C:
                            turn_adj((c + 1) % QUAD, adj_first_in if c + 1 < QUAD else adj_in, 1, c if c else None)
                        split_adj(c, c % 2, block_of(c))
                        if c in (C - 3, C - 2):
                            split_stationary(0, c - C + 3, c - C + 3)
                    for pair in range(2):
                        sum_pair(pair, 1)

                    def z_chunks(b):
                        for c in range(C):
                            dve.wait_ge(acc_free_act, b * STEPS + c + 3)
                            dve.tensor_tensor(zT_lo[:, c, :], acc[c % 2][:], zT_hi[:, c, :].bitcast(F32),
                                              ALU.subtract).then_inc(acc_free_dve, 1)
                            split_stationary((c // 2 + 1) % 2, c % 2, b * STEPS + c + 2)
                            if c in (1, 3):
                                sum_pair(c // 2 + 2, b * PAIRS + 2)
                            if c == 4:
                                dve.wait_ge(x_totals, b + 1)
                                dve.tensor_scalar(x_mean[:], p_router[:, 0:C], 1.0 / N, None,
                                                  ALU.mult).then_inc(x_means, 1)
                            if c == 5:
                                dve.wait_ge(scored, b + 1)
                                dve.tensor_tensor(scores[:], p_router[0:1, 64:64 + SCORES], r_b[:],
                                                  ALU.add).then_inc(router_dve, 1)
                                dve.wait_ge(router_dve, 2 * b + 1)
                                dve.sem_inc(carried, 1)
                                dve.max(best[:], scores[:]).then_inc(router_dve, 1)
                                dve.wait_ge(router_dve, 2 * b + 2)
                                dve.sem_inc(carried, 1)
                                dve.max_index(best_at[:], best[:], scores[:]).then_inc(chosen, 1)
                                dve.wait_ge(chosen, b + 1)
                                dve.tensor_copy(choice[0:1, bass.ds(b, 1)], best_at[0:1, 0:1])

                    def out_chunk(b, quad, j, split_next=True, adj_next=True):
                        c = quad * QUAD + j
                        if adj_next:
                            turn_adj(j, adj_in, b * 2 + 1 + quad + 1, b * C + C + c - 1)
                            split_adj(b * C + C + c, j % 2, bass.ds(c * P, P))
                        dve.wait_ge(acc_free_act, b * STEPS + C + c + 3)
                        for half in range(N // BANK):
                            last = dve.bn_stats(
                                stats[:, b, c, 2 * half:2 * half + 2, :].rearrange("p g s -> p (g s)"),
                                acc[j % 2][:, half * BANK:(half + 1) * BANK])
                        last.then_inc(acc_free_dve, 1)
                        if split_next:
                            split_stationary((j // 2 + 1) % 2, j % 2, b * STEPS + C + c + 2)

                    with dve.Fori(0, B - 1) as b:
                        z_chunks(b)
                        with dve.Fori(0, C // QUAD) as quad:
                            for j in range(QUAD):
                                out_chunk(b, quad, j)
                        for pair in range(2):
                            sum_pair(pair, b * PAIRS + PAIRS + 1)
                    z_chunks(B - 1)
                    for c in range(C):
                        out_chunk(B - 1, c // QUAD, c % QUAD, split_next=c < C - 2, adj_next=False)

        TILES_PS = 4
        STORES = 1
        STORED = 16 * STORES
        GROUP = N // 4

        with ExitStack() as ctx:
            def sb(name, shape, dt=F32):
                return ctx.enter_context(nc.sbuf_tensor(name, shape, dt))

            out_u += [sb(f"out_u{i}", [P, C, ROWS]) for i in range(EARLY, SLOTS)]
            x_u += [sb(f"x_u{i}", [P, TILES, H]) for i in range(EARLY, SLOTS)]
            tile_ps = [ctx.enter_context(nc.psum_tensor(f"tile_ps{i}", [P, K], F32)) for i in range(TILES_PS)]
            choice_all = sb("choice_all", [P, B])
            is_expert = sb("is_expert", [P, E, B])
            per_count = sb("per_count", [P, E])
            squares = sb("squares", [P, B, C, 4])
            sum_1, sum_2 = sb("sum_1", [P, B, C]), sb("sum_2", [P, B, C])
            masked = sb("masked", [P, E * B * C])
            mean, var = sb("mean", [P, E, C]), sb("var", [P, E, C])
            mean_sq = sb("mean_sq", [P, E, C])
            gamma_beta = sb("gamma_beta", [P, 2, E, C])
            scale, shift = sb("scale", [P, B, C]), sb("shift", [P, B, C])
            ln_stats = sb("ln_stats", [P, TILES, 2, 6])
            ln_var_eps = sb("ln_var_eps", [P, TILES])
            minus_half = sb("minus_half", [P, E, C])
            ln_mv = sb("ln_mv", [P, TILES, 2])
            ln_scale = [sb(f"ln_scale{i}", [P, TILES]) for i in range(SLOTS)]
            ln_shift = [sb(f"ln_shift{i}", [P, TILES]) for i in range(SLOTS)]

            y_stored = [sem(f"y_stored{i}") for i in range(SLOTS)]
            tables_in_ps = sem("tables_in_ps")
            bn_steps = sem("bn_steps")
            bn_ready = sem("bn_ready")
            relu_done = sem("relu_done")
            tile_turned = sem("tile_turned")
            tile_added = sem("tile_added")
            ln_taken = sem("ln_taken")
            half_ready = sem("half_ready")
            ln_aggregated = sem("ln_aggregated")
            bn_var = sem("bn_var")
            bn_inverse = sem("bn_inverse")
            ln_var = sem("ln_var")
            ln_inverse = sem("ln_inverse")
            ln_ready = sem("ln_ready")
            y_ready = sem("y_ready")

            with nc.Block() as block:
                @block.sync
                def _(sp):
                    for slot in range(EARLY, SLOTS):
                        load_unit(sp, slot // PER_GRAPH, slot % PER_GRAPH, slot, slot)
                    with sp.Fori(0, UNITS // SLOTS - 1) as i:
                        for slot in range(SLOTS):
                            sp.wait_ge(tile_turned, (i * SLOTS + slot + 1) * TILES)
                            sp.wait_ge(y_stored[slot], (i + 1) * STORED)
                            load_unit(sp, (i + 1) * (SLOTS // PER_GRAPH) + slot // PER_GRAPH, slot % PER_GRAPH,
                                      (i + 1) * SLOTS + slot, slot)

                @block.gpsimd
                def _(pool):
                    pool.memset(minus_half[:], -0.5).then_inc(half_ready, 1)
                    pool.wait_ge(half_ready, 1)
                    pool.wait_ge(bn_var, 1)
                    pool.tensor_tensor(var[:], var[:], minus_half[:], ALU.pow).then_inc(bn_inverse, 1)
                    with pool.Fori(0, UNITS // SLOTS) as i:
                        for slot in range(SLOTS):
                            pool.wait_ge(ln_var, i * SLOTS + slot + 1)
                            pool.tensor_tensor(ln_scale[slot][:], ln_var_eps[:], minus_half[:, 0, 0:TILES],
                                               ALU.pow).then_inc(ln_inverse, 1)

                @block.tensor
                def _(pe):
                    pe.matmul(tile_ps[3][:, 0:B], ones[0:1, :], choice[:], start=True, stop=True).then_inc(tables_in_ps, 1)
                    pe.wait_ge(gb_in, 32)
                    pe.transpose(tile_ps[3][:, BANK:BANK + GB], gb_rows[:], ident[0:GB, 0:GB]).then_inc(tables_in_ps, 1)
                    pe.wait_ge(bn_ready, 1)
                    with pe.Fori(0, UNITS // SLOTS) as i:
                        for slot in range(SLOTS):
                            pe.wait_ge(relu_done, i * SLOTS + slot + 1)
                            for t in range(TILES):
                                pe.wait_ge(tile_added, (i * SLOTS + slot) * TILES + t + 1)
                                ps = tile_ps[(slot * TILES + t) % TILES_PS]
                                for c in range(C):
                                    last = pe.transpose(ps[:, c * P:(c + 1) * P],
                                                        out_u[slot][:, c, t * P:(t + 1) * P], ident[:])
                                last.then_inc(tile_turned, 1)

                @block.scalar
                def _(act):
                    act.wait_ge(bn_ready, 1)

                    def relu(graph, slot, uses):
                        act.wait_ge(out_in[slot], 16 * uses)
                        act.sem_inc(carried, 1)
                        for c in range(C):
                            last = act.activation(out_u[slot][:, c, :], out_u[slot][:, c, :], ACT.Relu,
                                                  bias=shift[:, graph, c:c + 1], scale=scale[:, graph, c:c + 1])
                        last.then_inc(relu_done, 1)

                    def normalise_and_store(unit, slot):
                        act.wait_ge(ln_ready, unit + 1)
                        for part in range(STORES):
                            tiles = range(part * TILES // STORES, (part + 1) * TILES // STORES)
                            for t in tiles:
                                last = act.activation(x_u[slot][:, t, :], x_u[slot][:, t, :], ACT.Identity,
                                                      bias=ln_shift[slot][:, t:t + 1],
                                                      scale=ln_scale[slot][:, t:t + 1])
                            last.then_inc(y_ready, 1)
                            act.wait_ge(y_ready, unit * STORES + part + 1)
                            act.dma_start(y_units[unit][:, tiles.start:tiles.stop],
                                          x_u[slot][:, tiles.start:tiles.stop]).then_inc(y_stored[slot], 16)

                    relu(0, 0, 1)
                    with act.Fori(0, UNITS // SLOTS - 1) as i:
                        for slot in range(SLOTS):
                            ahead = slot + 1
                            relu(i * (SLOTS // PER_GRAPH) + ahead // PER_GRAPH, ahead % SLOTS, i + ahead // SLOTS + 1)
                            normalise_and_store(i * SLOTS + slot, slot)
                    for unit in range(UNITS - SLOTS, UNITS):
                        ahead = unit + 1
                        if ahead < UNITS:
                            relu(ahead // PER_GRAPH, ahead % SLOTS, ahead // SLOTS + 1)
                        normalise_and_store(unit, unit % SLOTS)
                    for s in y_stored:
                        act.wait_ge(s, STORED * (UNITS // SLOTS))

                @block.vector
                def _(dve):
                    done = [0]

                    def then(instruction):
                        done[0] += 1
                        instruction.then_inc(bn_steps, 1)
                        dve.wait_ge(bn_steps, done[0])

                    means, sq_devs = stats[:, :, :, :, 1], stats[:, :, :, :, 2]

                    dve.tensor_reduce(sum_1[:], means, AX_X, ALU.add)
                    then(dve.tensor_tensor(squares[:], means, means, ALU.mult))
                    then(dve.scalar_tensor_tensor(out=squares[:], in0=squares[:], scalar=float(GROUP), in1=sq_devs,
                                                  op0=ALU.mult, op1=ALU.add))
                    then(dve.tensor_reduce(sum_2[:], squares[:], AX_X, ALU.add))
                    dve.wait_ge(tables_in_ps, 1)
                    then(dve.tensor_copy(choice_all[:], tile_ps[3][:, 0:B]))
                    for e in range(E):
                        last = dve.tensor_scalar(is_expert[:, e, :], choice_all[:], float(e), None, ALU.is_equal)
                    then(last)
                    then(dve.tensor_reduce(per_count[:], is_expert[:], AX_X, ALU.add))
                    then(dve.tensor_scalar(per_count[:], per_count[:], float(N), 1.0, ALU.mult, ALU.max))
                    then(dve.reciprocal(per_count[:], per_count[:]))
                    by_expert = masked[:].rearrange("p (e b c) -> p e b c", e=E, b=B)
                    of_graph = is_expert[:].unsqueeze(3).to_broadcast([P, E, B, C])
                    count_of = per_count[:].unsqueeze(2).to_broadcast([P, E, C])
                    for total, moment, unit in ((sum_1, mean, float(GROUP)), (sum_2, var, 1.0)):
                        then(dve.tensor_tensor(by_expert, total[:].unsqueeze(1).to_broadcast([P, E, B, C]),
                                               of_graph, ALU.mult))
                        then(dve.tensor_reduce(moment[:], by_expert.rearrange("p e b c -> p e c b"), AX_X, ALU.add))
                        then(dve.scalar_tensor_tensor(out=moment[:], in0=moment[:], scalar=unit, in1=count_of,
                                                      op0=ALU.mult, op1=ALU.mult))
                    then(dve.tensor_tensor(mean_sq[:], mean[:], mean[:], ALU.mult))
                    then(dve.tensor_tensor(var[:], var[:], mean_sq[:], ALU.subtract))
                    dve.tensor_scalar(var[:], var[:], BN_EPS, None, ALU.add).then_inc(bn_var, 1)
                    dve.wait_ge(bn_inverse, 1)
                    dve.wait_ge(tables_in_ps, 2)
                    then(dve.tensor_copy(gamma_beta[:].rearrange("p g e c -> p (g e c)"),
                                         tile_ps[3][:, BANK:BANK + GB]))
                    then(dve.tensor_tensor(var[:], var[:], gamma_beta[:, 0], ALU.mult))
                    then(dve.tensor_tensor(mean[:], mean[:], var[:], ALU.mult))
                    then(dve.tensor_tensor(mean[:], gamma_beta[:, 1], mean[:], ALU.subtract))
                    by_graph = masked[:].rearrange("p (b c e) -> p b c e", e=E, b=B)
                    expert_of = is_expert[:].rearrange("p e b -> p b e").unsqueeze(2).to_broadcast([P, B, C, E])
                    for table, own in ((var, scale), (mean, shift)):
                        then(dve.tensor_tensor(by_graph, expert_of,
                                               table[:].rearrange("p e c -> p c e").unsqueeze(1).to_broadcast([P, B, C, E]),
                                               ALU.mult))
                        then(dve.tensor_reduce(own[:], by_graph, AX_X, ALU.add))
                    dve.sem_inc(tile_added, TILES_PS)
                    dve.sem_inc(bn_ready, 1)

                    with dve.Fori(0, UNITS // SLOTS) as i:
                        for slot in range(SLOTS):
                            unit = i * SLOTS + slot
                            dve.wait_ge(x_in[slot], (i + 1) * 16)
                            for t in range(TILES):
                                dve.wait_ge(tile_turned, unit * TILES + t + 1)
                                dve.tensor_tensor(x_u[slot][:, t, :], x_u[slot][:, t, :],
                                                  tile_ps[(slot * TILES + t) % TILES_PS][:],
                                                  ALU.add).then_inc(tile_added, 1)
                                dve.wait_ge(tile_added, unit * TILES + TILES_PS + t + 1)
                                for half in range(H // BANK):
                                    last = dve.bn_stats(ln_stats[:, t, half, :],
                                                        x_u[slot][:, t, half * BANK:(half + 1) * BANK])
                                last.then_inc(ln_taken, 1)
                            dve.wait_ge(ln_taken, unit * TILES + TILES)
                            dve.sem_inc(carried, 1)
                            for t in range(TILES):
                                last = dve.bn_aggr(ln_mv[:, t, :], ln_stats[:, t].rearrange("p a s -> p (a s)"))
                            last.then_inc(ln_aggregated, 1)
                            dve.wait_ge(ln_aggregated, unit + 1)
                            dve.tensor_scalar(ln_var_eps[:], ln_mv[:, :, 1], LN_EPS, None,
                                              ALU.add).then_inc(ln_var, 1)
                            dve.wait_ge(ln_inverse, unit + 1)
                            dve.scalar_tensor_tensor(out=ln_shift[slot][:], in0=ln_mv[:, :, 0], scalar=-1.0,
                                                     in1=ln_scale[slot][:], op0=ALU.mult,
                                                     op1=ALU.mult).then_inc(ln_ready, 1)


INPUTS = ["x", "adj", "L0_gnn_router_w", "L0_gnn_router_b", "L0_gnn_expert_w", "L0_gnn_bn_gamma", "L0_gnn_bn_beta"]


def kernel(**inputs):
    import numpy as np
    import concourse.bacc as bacc
    from concourse.bass_utils import run_bass_kernel_spmd

    nc = bacc.Bacc("TRN2", target_bir_lowering=False, num_devices=1)
    arrays, args = {}, []
    for name in INPUTS:
        a = np.ascontiguousarray(inputs[name])
        arrays[f"in_{name}"] = a
        args.append(nc.dram_tensor(f"in_{name}", a.shape, mybir.dt.from_np(a.dtype), kind="ExternalInput").ap())
    y = nc.dram_tensor("out_y", inputs["x"].shape, F32, kind="ExternalOutput").ap()
    graph_layer(nc, *args, y)
    return run_bass_kernel_spmd(nc, [arrays], core_ids=[0]).results[0]["out_y"]
```

```python
from contextlib import ExitStack

import concourse.bass as bass
from concourse import mybir

F32 = mybir.dt.float32
F32R = mybir.dt.float32r
U32 = mybir.dt.uint32
ALU = mybir.AluOpType
ACT = mybir.ActivationFunctionType
AX_X = mybir.AxisListType.X

P = 128
BANK = 512
BN_EPS = 1e-5
LN_EPS = 1e-5


def graph_layer(nc, x, adj, router_w, router_b, expert_w, bn_gamma, bn_beta, y):
    B, N, H = x.shape
    E = router_w.shape[1]
    K = expert_w.shape[2]
    C = H // P
    assert N == H == K and C == 8 and E == 4 and N == 2 * BANK
    STEPS = 2 * C
    PAIR = 2 * P
    PAIRS = C // 2
    PAIR_IN = 16 * 4
    QUAD = 4
    SCORES = 8
    GB = 2 * E * C

    QUADRANT = 32
    QUADS = P // QUADRANT
    adj_blocks = adj.rearrange("b (c i r) (j m) -> b c j r i m", i=QUADS, r=QUADRANT, j=QUADS)
    x_pairs = x.rearrange("b (j c r) (q h) -> b q j r c h", j=QUADS, r=QUADRANT, h=PAIR)
    w_pairs = expert_w.rearrange("e (c j r) (q k) -> e q j r c k", j=QUADS, r=QUADRANT, k=PAIR)
    outT = nc.dram_tensor("outT_scratch", (B, K, N), F32, kind="Internal").ap()
    outT_rows = outT.rearrange("b (c p) n -> b c p n", p=P)

    with ExitStack() as whole:
        def sem(name):
            return whole.enter_context(nc.semaphore(name))

        stats = whole.enter_context(nc.sbuf_tensor("stats", [P, B, C, 4, 3], F32))
        choice = whole.enter_context(nc.sbuf_tensor("choice", [1, B], F32))
        ones = whole.enter_context(nc.sbuf_tensor("ones", [P, P], F32))
        ident = whole.enter_context(nc.sbuf_tensor("ident", [P, P], F32))
        gb_rows = whole.enter_context(nc.sbuf_tensor("gb_rows", [GB, P], F32))
        choice_all = whole.enter_context(nc.sbuf_tensor("choice_all", [P, B], F32))
        gamma_beta = whole.enter_context(nc.sbuf_tensor("gamma_beta", [P, 2, E, C], F32))
        scale = whole.enter_context(nc.sbuf_tensor("scale", [P, B, C], F32))
        shift = whole.enter_context(nc.sbuf_tensor("shift", [P, B, C], F32))
        minus_half = whole.enter_context(nc.sbuf_tensor("minus_half", [P, E, C], F32))
        carried = sem("carried")
        gb_in = sem("gb_in")

        ROWS = 2 * P
        TILES = ROWS // P
        UNITS = B * N // ROWS
        PER_GRAPH = N // ROWS
        SLOTS = 8
        EARLY = 6

        outT_units = outT.rearrange("b (c p) (u n) -> b u p c n", p=P, n=ROWS)
        x_units = x.rearrange("b (u t p) h -> (b u) p t h", t=TILES, p=P)
        y_units = y.rearrange("b (u t p) h -> (b u) p t h", t=TILES, p=P)

        at = nc.sbuf_base
        KEPT = C * N * 4
        ROW = N * 4
        UNIT = C * ROWS * 4
        assert 2 * KEPT + (QUAD + 2) * ROW + C * PAIR * 4 == 2 * EARLY * UNIT
        whole.enter_context(nc.sbuf_tensor("adj_or_units", [P, 2 * EARLY * UNIT // 4], F32))
        adjT_hi = nc.alloc_sbuf_tensor_at("adjT_hi", [P, C, N], F32R, offset=at)
        adjT_lo = nc.alloc_sbuf_tensor_at("adjT_lo", [P, C, N], F32R, offset=at + KEPT)
        adj_raw = [nc.alloc_sbuf_tensor_at(f"adj_raw{i}", [P, QUADS, N // QUADS], F32,
                                           offset=at + 2 * KEPT + i * ROW) for i in range(QUAD)]
        turned = [nc.alloc_sbuf_tensor_at(f"turned{i}", [P, C, P], F32,
                                          offset=at + 2 * KEPT + (QUAD + i) * ROW) for i in range(2)]
        raw_0 = nc.alloc_sbuf_tensor_at("raw0", [P, C, PAIR], F32, offset=at + 2 * KEPT + (QUAD + 2) * ROW)
        out_u = [nc.alloc_sbuf_tensor_at(f"out_u{i}", [P, C, ROWS], F32, offset=at + 2 * i * UNIT)
                 for i in range(EARLY)]
        x_u = [nc.alloc_sbuf_tensor_at(f"x_u{i}", [P, TILES, H], F32, offset=at + (2 * i + 1) * UNIT)
               for i in range(EARLY)]
        out_in = [sem(f"out_in{i}") for i in range(SLOTS)]
        x_in = [sem(f"x_in{i}") for i in range(SLOTS)]

        out_stored = [sem(f"out_stored{i}") for i in range(2)]
        bn_ready = sem("bn_ready")

        def load_out(sp, graph, part, slot):
            sp.dma_start(out_u[slot][:], outT_units[graph, part]).then_inc(out_in[slot], 16)

        def load_x(sp, unit, slot):
            sp.dma_start(x_u[slot][:], x_units[unit]).then_inc(x_in[slot], 16)

        with ExitStack() as ctx:
            def sb(name, shape, dt=F32):
                return ctx.enter_context(nc.sbuf_tensor(name, shape, dt))

            def psum(name, shape):
                return ctx.enter_context(nc.psum_tensor(name, shape, F32))

            zT_hi, zT_lo = sb("zT_hi", [P, C, N], F32R), sb("zT_lo", [P, C, N], F32R)
            raw = [raw_0, sb("raw1", [P, C, PAIR])]
            st_hi = [sb(f"st_hi{i}", [P, C, P], F32R) for i in range(2)]
            st_lo = [sb(f"st_lo{i}", [P, C, P], F32R) for i in range(2)]
            out_sb = [sb(f"out_sb{i}", [P, N]) for i in range(2)]
            x_sums = sb("x_sums", [P, H])
            quadrant_sums = sb("quadrant_sums", [P, H // QUADRANT])
            r_w = sb("r_w", [P, H // QUADRANT, SCORES])
            shares = sb("shares", [P, SCORES])
            r_b = sb("r_b", [1, SCORES])
            scores = sb("scores", [1, SCORES])
            best = sb("best", [1, 8])
            best_at = sb("best_at", [1, 8], U32)
            is_expert = sb("is_expert", [P, E, B])
            per_count = sb("per_count", [P, E])
            sum_1, sum_2 = sb("sum_1", [P, B, C]), sb("sum_2", [P, B, C])
            mean, var = sb("mean", [P, E, C]), sb("var", [P, E, C])
            sums_turned = turned[0][:].rearrange("p c (q i) -> p (c q) i", i=QUADRANT)
            weighted = turned[1][:].rearrange("p (e c) h -> p e (c h)", e=SCORES)[:, :, 0:H // QUADRANT]
            assert 4 * B * C + E * B * C <= H
            squares = x_sums[:, 0:4 * B * C].rearrange("p (b c g) -> p b c g", b=B, c=C)
            masked = x_sums[:, 4 * B * C:4 * B * C + E * B * C]
            mean_sq = quadrant_sums[:, 0:E * C].rearrange("p (e c) -> p e c", e=E)

            acc = [psum(f"acc{i}", [P, N]) for i in range(2)]
            p_small = psum("p_small", [P, BANK])
            p_scores = p_small[0:1, 0:SCORES]
            p_choice, p_gb = p_small[:, 128:128 + B], p_small[:, 192:192 + GB]

            ones_ready = sem("ones_ready")
            ident_ready = sem("ident_ready")
            router_in = sem("router_in")
            raw_in = [sem(f"raw_in{i}") for i in range(2)]
            adj_in = [sem(f"adj_in{i}") for i in range(QUAD)]
            adj_first_in = [sem(f"adj_first_in{i}") for i in range(QUAD)]
            st_hi_ready = sem("st_hi_ready")
            st_lo_ready = sem("st_lo_ready")
            products_done = sem("products_done")
            acc_free_act = sem("acc_free_act")
            acc_free_dve = sem("acc_free_dve")
            adj_turned = sem("adj_turned")
            adjT_hi_ready = sem("adjT_hi_ready")
            adjT_lo_ready = sem("adjT_lo_ready")
            x_summed = sem("x_summed")
            shares_ready = sem("shares_ready")
            scored = sem("scored")
            router_dve = sem("router_dve")
            chosen = sem("chosen")
            choice_noted = sem("choice_noted")
            choice_spread = sem("choice_spread")
            half_ready = sem("half_ready")
            gb_turned = sem("gb_turned")
            bn_steps = sem("bn_steps")
            bn_var = sem("bn_var")
            bn_inverse = sem("bn_inverse")

            BN_PARTS = [slice(0, 5), slice(5, 7), slice(7, 8)]
            GROUP = N // 4

            with nc.Block() as block:
                @block.sync
                def _(sp):
                    def load_quadrants(tile, src, landed):
                        for j in range(QUADS):
                            sp.dma_start(tile[j * QUADRANT:(j + 1) * QUADRANT], src[j]).then_inc(landed, 16)

                    for c in range(QUAD):
                        load_quadrants(adj_raw[c], adj_blocks[0, c], adj_first_in[c])
                    for q in range(2):
                        load_quadrants(raw[q], x_pairs[0, q], raw_in[q])

                    def load(pair, step, src):
                        sp.wait_ge(st_hi_ready, step - 2)
                        sp.wait_ge(st_lo_ready, step - 2)
                        load_quadrants(raw[pair % 2], src, raw_in[pair % 2])

                    def load_graph(b):
                        for q in range(2, PAIRS):
                            sp.wait_ge(x_summed, b * PAIRS + q - 1)
                            sp.sem_inc(carried, 1)
                            load(q, b * STEPS + 2 * q, x_pairs[b, q])
                        sp.wait_ge(chosen, b + 1)
                        sp.sem_inc(carried, 1)
                        e = sp.value_load(best_at[0:1, 0:1], min_val=0, max_val=E - 1)
                        for q in range(PAIRS):
                            load(q, b * STEPS + C + 2 * q, w_pairs[e, q])

                    with sp.Fori(0, B - 1) as b:
                        load_graph(b)
                        for q in range(2):
                            load(q, b * STEPS + STEPS + 2 * q, x_pairs[b + 1, q])
                    load_graph(B - 1)

                    for s in out_stored:
                        sp.wait_ge(s, 16 * (2 * (C // 2) + 1))
                    for slot in range(EARLY):
                        sp.wait_ge(products_done, (B - 1) * STEPS + C + slot)
                        load_out(sp, slot // PER_GRAPH, slot % PER_GRAPH, slot)
                        if slot == EARLY - 1:
                            sp.wait_ge(st_hi_ready, (B - 1) * STEPS + 2 * C - 2)
                            sp.wait_ge(st_lo_ready, (B - 1) * STEPS + 2 * C - 2)
                        load_x(sp, slot, slot)

                @block.gpsimd
                def _(pool):
                    pool.memset(ones[:], 1.0).then_inc(ones_ready, 1)
                    pool.memset(ident[:], 0.0).then_inc(ident_ready, 1)
                    pool.wait_ge(ident_ready, 1)
                    pool.affine_select(out=ident[:], in_=ident[:], compare_op=ALU.not_equal, fill=1.0, base=0,
                                       pattern=[[-1, P]], channel_multiplier=1).then_inc(ident_ready, 1)
                    pool.memset(minus_half[:], -0.5).then_inc(half_ready, 1)

                    def load_adj(block_no, slot, src):
                        pool.wait_ge(adj_turned, block_no - QUAD + 1)
                        for j in range(QUADS):
                            pool.dma_start(adj_raw[slot][j * QUADRANT:(j + 1) * QUADRANT],
                                           src[j]).then_inc(adj_in[slot], 16)

                    for c in range(QUAD, C):
                        load_adj(c, c - QUAD, adj_blocks[0, c])
                    with pool.Fori(1, B) as b:
                        for c in range(C):
                            load_adj(b * C + c, c % QUAD, adj_blocks[b, c])
                    pool.wait_ge(half_ready, 1)
                    for part, chunks in enumerate(BN_PARTS):
                        pool.wait_ge(bn_var, part + 1)
                        pool.tensor_tensor(var[:, :, chunks], var[:, :, chunks], minus_half[:, :, chunks],
                                           ALU.pow).then_inc(bn_inverse, 1)

                @block.tensor
                def _(pe):
                    pe.wait_ge(ones_ready, 1)
                    pe.wait_ge(ident_ready, 2)

                    pe.wait_ge(gb_in, 32)
                    pe.transpose(p_gb, gb_rows[:], ident[0:GB, 0:GB]).then_inc(gb_turned, 1)

                    def operands_ready(step):
                        pe.wait_ge(st_hi_ready, step + 1)
                        pe.wait_ge(st_lo_ready, step + 1)
                        pe.wait_ge(acc_free_act, step + 1)
                        pe.wait_ge(acc_free_dve, step + 1)

                    def products(c, mv_hi, mv_lo, halves=(0, 1), before_last=None):
                        for t in range(C):
                            if t == C - 1 and before_last:
                                before_last()
                            for n, (st, mv) in enumerate(((st_hi, mv_hi), (st_hi, mv_lo), (st_lo, mv_hi))):
                                for half in halves:
                                    cols = slice(half * BANK, (half + 1) * BANK)
                                    last = pe.matmul(acc[c % 2][:, cols], st[c % 2][:, t, :], mv[:, t, cols],
                                                     start=(t == 0 and n == 0), stop=(t == C - 1 and n == 2))
                        return last

                    with pe.Fori(0, B) as b:
                        for half in range(2):
                            pe.wait_ge(adjT_hi_ready, b * C + (half + 1) * (C // 2))
                            pe.wait_ge(adjT_lo_ready, b * C + (half + 1) * (C // 2))
                            for c in range(2):
                                if half == 0:
                                    operands_ready(b * STEPS + c)
                                last = products(c, adjT_hi, adjT_lo, halves=(half,))
                                if half == 1:
                                    last.then_inc(products_done, 1)
                        for c in range(2, C):
                            if c == 6:
                                pe.wait_ge(shares_ready, b + 1)
                                pe.matmul(p_scores, ones[:, 0:1], shares[:], start=True, stop=True).then_inc(scored, 1)
                            operands_ready(b * STEPS + c)
                            products(c, adjT_hi, adjT_lo).then_inc(products_done, 1)

                        pe.wait_ge(choice_noted, b + 2)
                        pe.matmul(p_choice, ones[0:1, :], choice[:], start=True, stop=True).then_inc(choice_spread, 1)
                        with pe.Fori(0, C // QUAD) as quad:
                            for j in range(QUAD):
                                step = b * STEPS + C + quad * QUAD + j

                                def last_z():
                                    pe.wait_ge(acc_free_act, step + 2)
                                    pe.wait_ge(acc_free_dve, step + 2)
                                operands_ready(step)
                                products(j, zT_hi, zT_lo, before_last=last_z).then_inc(products_done, 1)

                def block_of(c):
                    return slice(c * P, (c + 1) * P)

                @block.scalar
                def _(act):
                    for n, table in enumerate((bn_gamma, bn_beta)):
                        act.dma_start(gb_rows[n * E * C:(n + 1) * E * C, :],
                                      table.rearrange("e (c p) -> (e c) p", p=P)).then_inc(gb_in, 16)
                    act.sem_inc(acc_free_act, 2)
                    for s in out_stored:
                        act.sem_inc(s, 16)

                    def split_adj(block_no, slot, cols):
                        act.wait_ge(adj_turned, block_no + 1)
                        act.activation(adjT_hi[:, :, cols], turned[slot][:], ACT.Copy).then_inc(adjT_hi_ready, 1)

                    def split_stationary(slot, half, uses):
                        if half == 0:
                            act.wait_ge(raw_in[slot], PAIR_IN * uses)
                        act.activation(st_hi[half][:], raw[slot][:, :, half * P:(half + 1) * P],
                                       ACT.Copy).then_inc(st_hi_ready, 1)

                    for c in range(C):
                        split_adj(c, c % 2, block_of(c))
                        if c == C // 2 - 1:
                            for half in range(2):
                                split_stationary(0, half, 1)
                            for j in range(QUADS):
                                act.dma_start(r_w[j * QUADRANT:(j + 1) * QUADRANT, :, 0:E],
                                              router_w.rearrange("(k r) e -> r k e", r=QUADRANT)).then_inc(router_in, 16)
                            act.dma_start(r_b[:, 0:E], router_b.rearrange("(a e) -> a e", a=1)).then_inc(router_in, 16)

                    def z_chunks(b):
                        for c in range(C):
                            act.wait_ge(products_done, b * STEPS + c + 1)
                            act.activation(zT_hi[:, c, :], acc[c % 2][:], ACT.Copy).then_inc(acc_free_act, 1)
                            pair = c // 2 + 1
                            split_stationary(pair % 2, c % 2, b * PAIRS + pair // 2 + 1)

                    def out_chunk(b, quad, j, split_next=True, adj_next=True):
                        c = quad * QUAD + j
                        if adj_next:
                            split_adj(b * C + C + c, j % 2, bass.ds(c * P, P))
                        act.wait_ge(out_stored[j % 2], (b * (C // 2) + quad * (QUAD // 2) + j // 2 + 1) * 16)
                        act.wait_ge(products_done, b * STEPS + C + c + 1)
                        act.activation(out_sb[j % 2][:], acc[j % 2][:], ACT.Copy).then_inc(acc_free_act, 1)
                        if split_next:
                            pair = j // 2 + 1
                            split_stationary(pair % 2, j % 2, b * PAIRS + PAIRS // 2 + quad + pair // 2 + 1)
                        act.wait_ge(acc_free_act, b * STEPS + C + c + 3)
                        act.dma_start(outT_rows[b, c], out_sb[j % 2][:]).then_inc(out_stored[j % 2], 16)

                    with act.Fori(0, B - 1) as b:
                        z_chunks(b)
                        with act.Fori(0, C // QUAD) as quad:
                            for j in range(QUAD):
                                out_chunk(b, quad, j)
                    z_chunks(B - 1)
                    for c in range(C):
                        out_chunk(B - 1, c // QUAD, c % QUAD, split_next=c < C - 2, adj_next=False)

                @block.vector
                def _(dve):
                    dve.sem_inc(acc_free_dve, 2)
                    dve.memset(choice[:], 0.0).then_inc(choice_noted, 1)

                    def turn_adj(slot, landed, uses, split_before=None):
                        if split_before is not None:
                            dve.wait_ge(adjT_lo_ready, split_before)
                        dve.wait_ge(landed[slot], PAIR_IN * uses)
                        dve.transpose(turned[slot % 2][:].rearrange("p c (i r) -> p c i r", r=QUADRANT),
                                      adj_raw[slot][:].rearrange("p i (c r) -> p c i r", r=QUADRANT)
                                      ).then_inc(adj_turned, 1)

                    def split_adj(block_no, slot, cols):
                        dve.wait_ge(adjT_hi_ready, block_no + 1)
                        dve.tensor_tensor(adjT_lo[:, :, cols], turned[slot][:], adjT_hi[:, :, cols].bitcast(F32),
                                          ALU.subtract).then_inc(adjT_lo_ready, 1)

                    def split_stationary(slot, half, step):
                        dve.wait_ge(st_hi_ready, step + 1)
                        dve.tensor_tensor(st_lo[half][:], raw[slot][:, :, half * P:(half + 1) * P],
                                          st_hi[half][:].bitcast(F32), ALU.subtract).then_inc(st_lo_ready, 1)

                    def sum_pair(pair, uses):
                        dve.wait_ge(raw_in[pair % 2], PAIR_IN * uses)
                        dve.tensor_reduce(x_sums[:, pair * PAIR:(pair + 1) * PAIR],
                                          raw[pair % 2][:].rearrange("p c h -> p h c"), AX_X,
                                          ALU.add).then_inc(x_summed, 1)

                    turn_adj(0, adj_first_in, 1)
                    for c in range(C):
                        if c == C // 2 - 1:
                            split_adj(c, c % 2, block_of(c))
                            split_stationary(0, 0, 0)
                            turn_adj((c + 1) % QUAD, adj_in, 1, c)
                            split_stationary(0, 1, 1)
                            continue
                        if c + 1 < C:
                            turn_adj((c + 1) % QUAD, adj_first_in if c + 1 < QUAD else adj_in, 1, c if c else None)
                        split_adj(c, c % 2, block_of(c))
                    for pair in range(2):
                        sum_pair(pair, 1)
                    dve.wait_ge(router_in, (QUADS + 1) * 16)
                    for e in range(E, SCORES):
                        dve.tensor_copy(r_w[:, :, e:e + 1], r_w[:, :, E - 1:E])
                        last = dve.tensor_copy(r_b[:, e:e + 1], r_b[:, E - 1:E])
                    last.then_inc(router_dve, 1)

                    def z_chunks(b):
                        for c in range(C):
                            dve.wait_ge(acc_free_act, b * STEPS + c + 3)
                            dve.tensor_tensor(zT_lo[:, c, :], acc[c % 2][:], zT_hi[:, c, :].bitcast(F32),
                                              ALU.subtract).then_inc(acc_free_dve, 1)
                            split_stationary((c // 2 + 1) % 2, c % 2, b * STEPS + c + 2)
                            if c in (1, 3):
                                sum_pair(c // 2 + 2, b * PAIRS + 2)
                            if c == 4:
                                dve.wait_ge(x_summed, b * PAIRS + PAIRS)
                                dve.wait_ge(adjT_lo_ready, b * C + C)
                                dve.transpose(sums_turned, x_sums[:].rearrange("p (k i) -> p k i", i=QUADRANT)
                                              ).then_inc(router_dve, 1)
                                dve.wait_ge(router_dve, 5 * b + 2)
                                dve.tensor_reduce(quadrant_sums[:], sums_turned, AX_X, ALU.add).then_inc(router_dve, 1)
                                dve.wait_ge(router_dve, 5 * b + 3)
                                dve.tensor_tensor(weighted, r_w[:].rearrange("p k e -> p e k"),
                                                  quadrant_sums[:].unsqueeze(1).to_broadcast([P, SCORES, H // QUADRANT]),
                                                  ALU.mult).then_inc(router_dve, 1)
                                dve.wait_ge(router_dve, 5 * b + 4)
                                dve.tensor_reduce(shares[:], weighted, AX_X, ALU.add).then_inc(shares_ready, 1)
                            if c == 5:
                                dve.wait_ge(scored, b + 1)
                                dve.scalar_tensor_tensor(out=scores[:], in0=p_scores, scalar=1.0 / N, in1=r_b[:],
                                                         op0=ALU.mult, op1=ALU.add).then_inc(router_dve, 1)
                                dve.wait_ge(router_dve, 5 * b + 5)
                                dve.sem_inc(carried, 1)
                                dve.max(best[:], scores[:]).then_inc(router_dve, 1)
                                dve.wait_ge(router_dve, 5 * b + 6)
                                dve.sem_inc(carried, 1)
                                dve.max_index(best_at[:], best[:], scores[:]).then_inc(chosen, 1)
                                dve.wait_ge(chosen, b + 1)
                                dve.tensor_copy(choice[0:1, bass.ds(b, 1)],
                                                best_at[0:1, 0:1]).then_inc(choice_noted, 1)

                    def out_chunk(b, quad, j, split_next=True, adj_next=True):
                        c = quad * QUAD + j
                        if adj_next:
                            turn_adj(j, adj_in, b * 2 + 1 + quad + 1, b * C + C + c - 1)
                            split_adj(b * C + C + c, j % 2, bass.ds(c * P, P))
                        dve.wait_ge(acc_free_act, b * STEPS + C + c + 3)
                        for half in range(N // BANK):
                            last = dve.bn_stats(
                                stats[:, b, c, 2 * half:2 * half + 2, :].rearrange("p g s -> p (g s)"),
                                acc[j % 2][:, half * BANK:(half + 1) * BANK])
                        last.then_inc(acc_free_dve, 1)
                        if split_next:
                            split_stationary((j // 2 + 1) % 2, j % 2, b * STEPS + C + c + 2)

                    with dve.Fori(0, B - 1) as b:
                        z_chunks(b)
                        with dve.Fori(0, C // QUAD) as quad:
                            for j in range(QUAD):
                                out_chunk(b, quad, j)
                        for pair in range(2):
                            sum_pair(pair, b * PAIRS + PAIRS + 1)
                    z_chunks(B - 1)

                    done = [0]

                    def then(instruction):
                        done[0] += 1
                        instruction.then_inc(bn_steps, 1)
                        dve.wait_ge(bn_steps, done[0])

                    def experts_of_graphs():
                        dve.wait_ge(choice_spread, B)
                        then(dve.tensor_copy(choice_all[:], p_choice))
                        for e in range(E):
                            last = dve.tensor_scalar(is_expert[:, e, :], choice_all[:], float(e), None, ALU.is_equal)
                        then(last)
                        then(dve.tensor_reduce(per_count[:], is_expert[:], AX_X, ALU.add))
                        then(dve.tensor_scalar(per_count[:], per_count[:], float(N), 1.0, ALU.mult, ALU.max))
                        then(dve.reciprocal(per_count[:], per_count[:]))
                        dve.wait_ge(gb_turned, 1)
                        then(dve.tensor_copy(gamma_beta[:].rearrange("p g e c -> p (g e c)"), p_gb))

                    def batch_norm_factors(part):
                        chunks = BN_PARTS[part]
                        W = chunks.stop - chunks.start
                        means, sq_devs = stats[:, :, chunks, :, 1], stats[:, :, chunks, :, 2]
                        squares_, sum_1_, sum_2_ = squares[:, :, chunks], sum_1[:, :, chunks], sum_2[:, :, chunks]
                        mean_, var_, mean_sq_ = mean[:, :, chunks], var[:, :, chunks], mean_sq[:, :, chunks]

                        dve.wait_ge(acc_free_dve, (B - 1) * STEPS + C + chunks.stop + 2)
                        dve.tensor_reduce(sum_1_, means, AX_X, ALU.add)
                        then(dve.tensor_tensor(squares_, means, means, ALU.mult))
                        then(dve.scalar_tensor_tensor(out=squares_, in0=squares_, scalar=float(GROUP), in1=sq_devs,
                                                      op0=ALU.mult, op1=ALU.add))
                        then(dve.tensor_reduce(sum_2_, squares_, AX_X, ALU.add))
                        products_ = masked[:, 0:E * B * W]
                        by_expert = products_.rearrange("p (e b c) -> p e b c", e=E, b=B)
                        of_graph = is_expert[:].unsqueeze(3).to_broadcast([P, E, B, W])
                        count_of = per_count[:].unsqueeze(2).to_broadcast([P, E, W])
                        for total, moment, unit in ((sum_1_, mean_, float(GROUP)), (sum_2_, var_, 1.0)):
                            then(dve.tensor_tensor(by_expert, total.unsqueeze(1).to_broadcast([P, E, B, W]),
                                                   of_graph, ALU.mult))
                            then(dve.tensor_reduce(moment, by_expert.rearrange("p e b c -> p e c b"), AX_X, ALU.add))
                            then(dve.scalar_tensor_tensor(out=moment, in0=moment, scalar=unit, in1=count_of,
                                                          op0=ALU.mult, op1=ALU.mult))
                        then(dve.tensor_tensor(mean_sq_, mean_, mean_, ALU.mult))
                        then(dve.tensor_tensor(var_, var_, mean_sq_, ALU.subtract))
                        dve.tensor_scalar(var_, var_, BN_EPS, None, ALU.add).then_inc(bn_var, 1)
                        dve.wait_ge(bn_inverse, part + 1)
                        then(dve.tensor_tensor(var_, var_, gamma_beta[:, 0, :, chunks], ALU.mult))
                        then(dve.tensor_tensor(mean_, mean_, var_, ALU.mult))
                        then(dve.tensor_tensor(mean_, gamma_beta[:, 1, :, chunks], mean_, ALU.subtract))
                        by_graph = products_.rearrange("p (b c e) -> p b c e", e=E, b=B)
                        expert_of = is_expert[:].rearrange("p e b -> p b e").unsqueeze(2).to_broadcast([P, B, W, E])
                        for table, own in ((var_, scale), (mean_, shift)):
                            then(dve.tensor_tensor(by_graph, expert_of,
                                                   table.rearrange("p e c -> p c e").unsqueeze(1).to_broadcast([P, B, W, E]),
                                                   ALU.mult))
                            then(dve.tensor_reduce(own[:, :, chunks], by_graph, AX_X, ALU.add))
                        dve.sem_inc(bn_ready, 1)

                    for c in range(C):
                        out_chunk(B - 1, c // QUAD, c % QUAD, split_next=c < C - 2, adj_next=False)
                        if c == 0:
                            experts_of_graphs()
                        for part, chunks in enumerate(BN_PARTS):
                            if chunks.stop == c + 1:
                                batch_norm_factors(part)

        TILES_PS = 4

        with ExitStack() as ctx:
            def sb(name, shape, dt=F32):
                return ctx.enter_context(nc.sbuf_tensor(name, shape, dt))

            out_u += [sb(f"out_u{i}", [P, C, ROWS]) for i in range(EARLY, SLOTS)]
            x_u += [sb(f"x_u{i}", [P, TILES, H]) for i in range(EARLY, SLOTS)]
            tile_ps = [ctx.enter_context(nc.psum_tensor(f"tile_ps{i}", [P, K], F32)) for i in range(TILES_PS)]
            ln_stats = sb("ln_stats", [P, TILES, 2, 6])
            ln_var_eps = sb("ln_var_eps", [P, TILES])
            ln_mv = sb("ln_mv", [P, TILES, 2])
            ln_scale = [sb(f"ln_scale{i}", [P, TILES]) for i in range(SLOTS)]
            ln_shift = [sb(f"ln_shift{i}", [P, TILES]) for i in range(SLOTS)]

            y_stored = [sem(f"y_stored{i}") for i in range(SLOTS)]
            relu_done = sem("relu_done")
            tile_turned = sem("tile_turned")
            tile_added = sem("tile_added")
            ln_taken = sem("ln_taken")
            ln_aggregated = sem("ln_aggregated")
            ln_var = sem("ln_var")
            ln_inverse = sem("ln_inverse")
            ln_ready = sem("ln_ready")
            y_ready = sem("y_ready")

            with nc.Block() as block:
                @block.sync
                def _(sp):
                    for s in out_stored:
                        sp.wait_ge(s, 16 * (B * C // 2 + 1))
                    for slot in range(EARLY, SLOTS):
                        load_out(sp, slot // PER_GRAPH, slot % PER_GRAPH, slot)
                        load_x(sp, slot, slot)
                    with sp.Fori(0, UNITS // SLOTS - 1) as i:
                        for slot in range(SLOTS):
                            sp.wait_ge(tile_turned, (i * SLOTS + slot + 1) * TILES)
                            load_out(sp, (i + 1) * (SLOTS // PER_GRAPH) + slot // PER_GRAPH, slot % PER_GRAPH, slot)
                            sp.wait_ge(y_stored[slot], (i + 1) * 16)
                            load_x(sp, (i + 1) * SLOTS + slot, slot)

                @block.gpsimd
                def _(pool):
                    with pool.Fori(0, UNITS // SLOTS) as i:
                        for slot in range(SLOTS):
                            pool.wait_ge(ln_var, i * SLOTS + slot + 1)
                            pool.tensor_tensor(ln_scale[slot][:], ln_var_eps[:], minus_half[:, 0, 0:TILES],
                                               ALU.pow).then_inc(ln_inverse, 1)

                @block.tensor
                def _(pe):
                    with pe.Fori(0, UNITS // SLOTS) as i:
                        for slot in range(SLOTS):
                            pe.wait_ge(relu_done, i * SLOTS + slot + 1)
                            for t in range(TILES):
                                pe.wait_ge(tile_added, (i * SLOTS + slot) * TILES + t + 1)
                                ps = tile_ps[(slot * TILES + t) % TILES_PS]
                                for c in range(C):
                                    last = pe.transpose(ps[:, c * P:(c + 1) * P],
                                                        out_u[slot][:, c, t * P:(t + 1) * P], ident[:])
                                last.then_inc(tile_turned, 1)

                @block.scalar
                def _(act):
                    act.wait_ge(bn_ready, len(BN_PARTS))

                    def relu(graph, slot, uses):
                        act.wait_ge(out_in[slot], 16 * uses)
                        act.sem_inc(carried, 1)
                        for c in range(C):
                            last = act.activation(out_u[slot][:, c, :], out_u[slot][:, c, :], ACT.Relu,
                                                  bias=shift[:, graph, c:c + 1], scale=scale[:, graph, c:c + 1])
                        last.then_inc(relu_done, 1)

                    def normalise_and_store(unit, slot):
                        act.wait_ge(ln_ready, unit + 1)
                        for t in range(TILES):
                            last = act.activation(x_u[slot][:, t, :], x_u[slot][:, t, :], ACT.Identity,
                                                  bias=ln_shift[slot][:, t:t + 1], scale=ln_scale[slot][:, t:t + 1])
                        last.then_inc(y_ready, 1)
                        act.wait_ge(y_ready, unit + 1)
                        act.dma_start(y_units[unit], x_u[slot][:]).then_inc(y_stored[slot], 16)

                    relu(0, 0, 1)
                    with act.Fori(0, UNITS // SLOTS - 1) as i:
                        for slot in range(SLOTS):
                            ahead = slot + 1
                            relu(i * (SLOTS // PER_GRAPH) + ahead // PER_GRAPH, ahead % SLOTS, i + ahead // SLOTS + 1)
                            normalise_and_store(i * SLOTS + slot, slot)
                    for unit in range(UNITS - SLOTS, UNITS):
                        ahead = unit + 1
                        if ahead < UNITS:
                            relu(ahead // PER_GRAPH, ahead % SLOTS, ahead // SLOTS + 1)
                        normalise_and_store(unit, unit % SLOTS)
                    for s in y_stored:
                        act.wait_ge(s, 16 * (UNITS // SLOTS))

                @block.vector
                def _(dve):
                    dve.sem_inc(tile_added, TILES_PS)

                    with dve.Fori(0, UNITS // SLOTS) as i:
                        for slot in range(SLOTS):
                            unit = i * SLOTS + slot
                            dve.wait_ge(x_in[slot], (i + 1) * 16)
                            for t in range(TILES):
                                dve.wait_ge(tile_turned, unit * TILES + t + 1)
                                dve.tensor_tensor(x_u[slot][:, t, :], x_u[slot][:, t, :],
                                                  tile_ps[(slot * TILES + t) % TILES_PS][:],
                                                  ALU.add).then_inc(tile_added, 1)
                                dve.wait_ge(tile_added, unit * TILES + TILES_PS + t + 1)
                                for half in range(H // BANK):
                                    last = dve.bn_stats(ln_stats[:, t, half, :],
                                                        x_u[slot][:, t, half * BANK:(half + 1) * BANK])
                                last.then_inc(ln_taken, 1)
                            dve.wait_ge(ln_taken, unit * TILES + TILES)
                            dve.sem_inc(carried, 1)
                            for t in range(TILES):
                                last = dve.bn_aggr(ln_mv[:, t, :], ln_stats[:, t].rearrange("p a s -> p (a s)"))
                            last.then_inc(ln_aggregated, 1)
                            dve.wait_ge(ln_aggregated, unit + 1)
                            dve.tensor_scalar(ln_var_eps[:], ln_mv[:, :, 1], LN_EPS, None,
                                              ALU.add).then_inc(ln_var, 1)
                            dve.wait_ge(ln_inverse, unit + 1)
                            dve.scalar_tensor_tensor(out=ln_shift[slot][:], in0=ln_mv[:, :, 0], scalar=-1.0,
                                                     in1=ln_scale[slot][:], op0=ALU.mult,
                                                     op1=ALU.mult).then_inc(ln_ready, 1)


INPUTS = ["x", "adj", "L0_gnn_router_w", "L0_gnn_router_b", "L0_gnn_expert_w", "L0_gnn_bn_gamma", "L0_gnn_bn_beta"]


def kernel(**inputs):
    import numpy as np
    import concourse.bacc as bacc
    from concourse.bass_utils import run_bass_kernel_spmd

    nc = bacc.Bacc("TRN2", target_bir_lowering=False, num_devices=1)
    arrays, args = {}, []
    for name in INPUTS:
        a = np.ascontiguousarray(inputs[name])
        arrays[f"in_{name}"] = a
        args.append(nc.dram_tensor(f"in_{name}", a.shape, mybir.dt.from_np(a.dtype), kind="ExternalInput").ap())
    y = nc.dram_tensor("out_y", inputs["x"].shape, F32, kind="ExternalOutput").ap()
    graph_layer(nc, *args, y)
    return run_bass_kernel_spmd(nc, [arrays], core_ids=[0]).results[0]["out_y"]
```
